# Optimizing a Trainium2 kernel written in Bass

```python
import numpy as np
import jax
import jax.numpy as jnp

def _softmax(x, axis=-1):
    return jax.nn.softmax(x, axis=axis)

def _gelu(x):
    return jax.nn.gelu(x, approximate=True)

def _silu(x):
    return jax.nn.silu(x)

def _sigmoid(x):
    return jax.nn.sigmoid(x)

def _layernorm(x, axis=-1, eps=1e-05):
    m = jnp.mean(x, axis=axis, keepdims=True)
    v = jnp.var(x, axis=axis, keepdims=True)
    return (x - m) / jnp.sqrt(v + eps)

def _scatter_add(tgt, idx, src, axis=0):
    return tgt.at[idx].add(src)

def _segment_sum(src, seg, n):
    return jax.ops.segment_sum(src, seg, n)
kernel_name = 'mk_conv_attn_hybrid_d2_conv_nchw256_r4_1123e7'

def setup_inputs(seed: int=0):
    np.random.seed(seed)
    _w = jnp.asarray

    def _rec_inputs():
        import jax
        import jax.numpy as jnp
        _gk = jax.random.key(seed)
        x = -0.0002928 + 1 * jax.random.normal(jax.random.fold_in(_gk, 1), (4, 64, 16, 16), jnp.float32)
        return x
    x = _rec_inputs()

    def _L0_conv_setup():
        import jax, jax.numpy as jnp
        import numpy as np
        HEADS = 4
        HEAD_DIM = 32
        DIM = 64
        EPS = 1e-12
        key = jax.random.key(seed)
        ks = jax.random.split(key, 5)
        inner = HEADS * HEAD_DIM
        x = jax.random.normal(ks[0], (4, DIM, 16, 16), dtype=jnp.float32)
        g = jax.random.normal(ks[1], (DIM,), dtype=jnp.float32) * 0.02 + 1.0
        w_qkv = jax.random.normal(ks[2], (3 * inner, DIM), dtype=jnp.float32) * DIM ** (-0.5)
        w_out = jax.random.normal(ks[3], (DIM, inner), dtype=jnp.float32) * inner ** (-0.5)
        b_out = jax.random.normal(ks[4], (DIM,), dtype=jnp.float32) * 0.01
        return {'x': x, 'g': g, 'w_qkv': w_qkv, 'w_out': w_out, 'b_out': b_out}
    _L0_conv_all = _L0_conv_setup()
    _L0_conv_in = {k: v for k, v in _L0_conv_all.items() if k in ('g', 'w_qkv', 'w_out', 'b_out')}
    del _L0_conv_all

    def _L1_attn_setup():
        import jax, jax.numpy as jnp
        import numpy as np
        EMBD = 64
        HEAD = 4
        HEAD_DIM = EMBD // HEAD
        key = jax.random.key(seed)
        ks = jax.random.split(key, 5)
        B, S = (16, 256)
        scale = 1.0 / np.sqrt(EMBD)
        return {'x': jax.random.normal(ks[0], (B, S, EMBD), dtype=jnp.float32), 'W_qkv': jax.random.normal(ks[1], (EMBD, 3 * EMBD), dtype=jnp.float32) * scale, 'b_qkv': jax.random.normal(ks[2], (3 * EMBD,), dtype=jnp.float32) * 0.01, 'W_out': jax.random.normal(ks[3], (EMBD, EMBD), dtype=jnp.float32) * scale, 'b_out': jax.random.normal(ks[4], (EMBD,), dtype=jnp.float32) * 0.01}
    _L1_attn_all = _L1_attn_setup()
    _L1_attn_in = {k: v for k, v in _L1_attn_all.items() if k in ('W_qkv', 'b_qkv', 'W_out', 'b_out')}
    del _L1_attn_all

    def _L1_ffn_setup():
        import jax, jax.numpy as jnp
        import numpy as np
        TOP_K = 2
        key = jax.random.key(seed)
        ks = jax.random.split(key, 4)
        B, L, D, H, E = (8, 1024, 64, 256, 8)
        s = 0.02
        return {'x': jax.random.normal(ks[0], (B, L, D), jnp.float32), 'Wg': jax.random.normal(ks[1], (D, E), jnp.float32) * s, 'bg': jnp.zeros((E,), jnp.float32), 'W1': jax.random.normal(ks[2], (E, D, H), jnp.float32) * s, 'b1': jnp.zeros((E, H), jnp.float32), 'W2': jax.random.normal(ks[3], (E, H, D), jnp.float32) * s, 'b2': jnp.zeros((E, D), jnp.float32)}
    _L1_ffn_all = _L1_ffn_setup()
    _L1_ffn_in = {k: v for k, v in _L1_ffn_all.items() if k in ('Wg', 'bg', 'W1', 'b1', 'W2', 'b2')}
    del _L1_ffn_all
    return {'x': x, 'L0_conv_g': _L0_conv_in['g'], 'L0_conv_w_qkv': _L0_conv_in['w_qkv'], 'L0_conv_w_out': _L0_conv_in['w_out'], 'L0_conv_b_out': _L0_conv_in['b_out'], 'L1_attn_W_qkv': _L1_attn_in['W_qkv'], 'L1_attn_b_qkv': _L1_attn_in['b_qkv'], 'L1_attn_W_out': _L1_attn_in['W_out'], 'L1_attn_b_out': _L1_attn_in['b_out'], 'L1_ffn_Wg': _L1_ffn_in['Wg'], 'L1_ffn_bg': _L1_ffn_in['bg'], 'L1_ffn_W1': _L1_ffn_in['W1'], 'L1_ffn_b1': _L1_ffn_in['b1'], 'L1_ffn_W2': _L1_ffn_in['W2'], 'L1_ffn_b2': _L1_ffn_in['b2']}

def reference(x, L0_conv_g, L0_conv_w_qkv, L0_conv_w_out, L0_conv_b_out, L1_attn_W_qkv, L1_attn_b_qkv, L1_attn_W_out, L1_attn_b_out, L1_ffn_Wg, L1_ffn_bg, L1_ffn_W1, L1_ffn_b1, L1_ffn_W2, L1_ffn_b2):
    import jax
    import jax.numpy as jnp

    def _L0_conv_ref(x, g, w_qkv, w_out, b_out):
        import jax, jax.numpy as jnp
        import numpy as np
        HEADS = 4
        HEAD_DIM = 32
        DIM = 64
        EPS = 1e-12
        b, c, h, w = x.shape
        n = h * w
        xn = x * jax.lax.rsqrt(jnp.mean(x * x, axis=1, keepdims=True) + EPS) * g[None, :, None, None]
        qkv = jnp.einsum('bchw,oc->bohw', xn, w_qkv)
        q, k, v = jnp.split(qkv, 3, axis=1)

        def to_bhnd(t):
            return t.reshape(b, HEADS, HEAD_DIM, n).transpose(0, 1, 3, 2)
        q, k, v = (to_bhnd(q), to_bhnd(k), to_bhnd(v))
        scale = HEAD_DIM ** (-0.5)
        sim = jnp.einsum('bhid,bhjd->bhij', q, k) * scale
        attn = jax.nn.softmax(sim, axis=-1)
        out = jnp.einsum('bhij,bhjd->bhid', attn, v)
        out = out.transpose(0, 1, 3, 2).reshape(b, HEADS * HEAD_DIM, h, w)
        return jnp.einsum('bchw,oc->bohw', out, w_out) + b_out[None, :, None, None]

    def _L1_attn_ref(x, W_qkv, b_qkv, W_out, b_out):
        import jax, jax.numpy as jnp
        import numpy as np
        EMBD = 64
        HEAD = 4
        HEAD_DIM = EMBD // HEAD
        B, S, E = x.shape
        qkv = x @ W_qkv + b_qkv
        q, k, v = jnp.split(qkv, 3, axis=-1)
        q = q.reshape(B, S, HEAD, HEAD_DIM).transpose(0, 2, 1, 3)
        k = k.reshape(B, S, HEAD, HEAD_DIM).transpose(0, 2, 1, 3)
        v = v.reshape(B, S, HEAD, HEAD_DIM).transpose(0, 2, 1, 3)
        att = jnp.einsum('bhqd,bhkd->bhqk', q, k) / jnp.sqrt(jnp.float32(HEAD_DIM))
        causal = jnp.tril(jnp.ones((S, S), dtype=bool))
        att = jnp.where(causal, att, -jnp.inf)
        att = jax.nn.softmax(att, axis=-1)
        out = jnp.einsum('bhqk,bhkd->bhqd', att, v)
        out = out.transpose(0, 2, 1, 3).reshape(B, S, E)
        return out @ W_out + b_out

    def _L1_ffn_ref(x, Wg, bg, W1, b1, W2, b2):
        import jax, jax.numpy as jnp
        import numpy as np
        TOP_K = 2
        B, L, D = x.shape
        E = W1.shape[0]
        xf = x.reshape(-1, D)
        gate_logits = xf @ Wg + bg
        top_w, top_i = jax.lax.top_k(gate_logits, TOP_K)
        top_w = jax.nn.softmax(top_w, axis=-1)
        w_dense = jnp.sum(jax.nn.one_hot(top_i, E, dtype=xf.dtype) * top_w[..., None], axis=1)
        out = jnp.zeros_like(xf)
        for e in range(E):
            h = jax.nn.gelu(xf @ W1[e] + b1[e], approximate=False)
            out = out + w_dense[:, e:e + 1] * (h @ W2[e] + b2[e])
        return out.reshape(B, L, D)

    def _gn(v, G=32, eps=1e-05):
        B_, C_, H_, W_ = v.shape
        g = v.reshape(B_, G, C_ // G, H_, W_)
        m = jnp.mean(g, axis=(2, 3, 4), keepdims=True)
        s = jnp.var(g, axis=(2, 3, 4), keepdims=True)
        return ((g - m) / jnp.sqrt(s + eps)).reshape(v.shape)

    def _ln_c(v, eps=1e-06):
        m = jnp.mean(v, axis=1, keepdims=True)
        s = jnp.var(v, axis=1, keepdims=True)
        return (v - m) / jnp.sqrt(s + eps)

    def _ln_t(v, eps=1e-05):
        m = jnp.mean(v, axis=-1, keepdims=True)
        s = jnp.var(v, axis=-1, keepdims=True)
        return (v - m) / jnp.sqrt(s + eps)

    def _to_tokens(v):
        B_, C_, H_, W_ = v.shape
        return v.reshape(B_, C_, H_ * W_).transpose(0, 2, 1)

    def _from_tokens(t, like):
        B_, C_, H_, W_ = like.shape
        return t.transpose(0, 2, 1).reshape(B_, C_, H_, W_)
    x = x + _L0_conv_ref(_gn(x), L0_conv_g, L0_conv_w_qkv, L0_conv_w_out, L0_conv_b_out)
    t = _to_tokens(x)
    t = t + _L1_attn_ref(_ln_t(t), L1_attn_W_qkv, L1_attn_b_qkv, L1_attn_W_out, L1_attn_b_out)
    t = t + _L1_ffn_ref(_ln_t(t), L1_ffn_Wg, L1_ffn_bg, L1_ffn_W1, L1_ffn_b1, L1_ffn_W2, L1_ffn_b2)
    x = _from_tokens(t, x)
    return x

_drawn_inputs = setup_inputs


def setup_inputs(seed=0):
    import zlib

    import numpy as np

    out = dict(_drawn_inputs(seed))
    spreads = {'L1_ffn_bg': (0.0, 0.413), 'L1_ffn_b1': (0.0, 2.0), 'L1_ffn_b2': (0.0, 0.628)}
    factors = {'L0_conv_g': 5.889,
     'L0_conv_b_out': 32.844,
     'L1_attn_b_qkv': 29.685,
     'L1_attn_b_out': 32.614,
     'L1_ffn_W1': 14.0,
     'L1_ffn_Wg': 2.725}
    for name, (base, spread) in spreads.items():
        noise = np.random.default_rng([zlib.crc32(name.encode()), seed]).standard_normal(out[name].shape)
        drawn = base * np.exp(spread * noise) if base else spread * noise
        out[name] = jnp.asarray(drawn.astype(out[name].dtype))
    for name, factor in factors.items():
        out[name] = (out[name] * factor).astype(out[name].dtype)
    return out
```

```python
from contextlib import ExitStack

import concourse.bass as bass
from concourse import mybir

F32 = mybir.dt.float32
F32R = mybir.dt.float32r
BF16 = mybir.dt.bfloat16
U32 = mybir.dt.uint32
ALU = mybir.AluOpType
ACT = mybir.ActivationFunctionType
AX = mybir.AxisListType

P = 128
MASKED = -1e30


def schedule(batches, lag):
    chain = [(step, layer) for layer in (0, 1) for step in ("norm", "project", "maxima", "probs", "out")]
    chain += [("norm", 2)]
    order = []
    for t in range(len(chain) + lag * (batches - 1)):
        for b in range(batches):
            if 0 <= t - lag * b < len(chain):
                step, layer = chain[t - lag * b]
                order.append((step, layer, b))
    return order


def hybrid_block(nc, x, g0, wqkv0, wout0, bout0, wqkv1, bqkv1, wout1, bout1, wg, bg, w1, b1, w2, b2, out):
    B, C, HH, WW = x.shape
    T = HH * WW
    H = 4
    D0 = wqkv0.shape[0] // 3 // H
    D1 = wqkv1.shape[1] // 3 // H
    E, _, F = w1.shape
    KT = T // P
    HP = H // 2
    FT = F // P
    NK = E * FT
    TT = B * T // P
    HALF = B * T // 2
    assert (B, C, T, H, D0, D1, E, F) == (4, 64, 256, 4, 32, 16, 8, 256)
    SCALE = (float(D0) ** -0.5, float(D1) ** -0.5)
    EPS = (1e-12, 1e-5, 1e-5)
    GN_EPS = 1e-5
    ORDER = schedule(B, 2)

    use, used = {}, [0] * 8

    def take(key, bank):
        use[key] = (bank, used[bank])
        used[bank] += 1

    for h in range(H):
        take(("prep_m", h), h)
    take("prep_t", 4)
    take("group", 5)
    ring, turn = list(range(8)), 0
    for step, layer, b in ORDER:
        names = {
            "norm": ["mean", "var"] if layer else ["var"],
            "project": ["y0", "y1", "v"],
            "maxima": ["s0", "s1", "s2", "s3"],
            "probs": ["t0", "t1", "t2", "t3"],
            "out": ["pv", "o"],
        }[step]
        for name in names:
            take((name, layer, b), ring[turn % 8])
            turn += 1
    ring_used = list(used)
    for k in range(NK):
        take(("h", k), 2 * (k % 2))
    take("gate", 6)
    take("gate_t", 7)
    for e in range(E):
        take(("y", e), 4 + e % 2)
        take(("w", e), 6 + e % 2)

    projections = [(l, b) for step, l, b in ORDER if step == "project"]
    number = {key: n for n, key in enumerate(projections)}
    before = dict(zip(projections[1:], projections))

    with ExitStack() as ctx:
        def sb(name, shape, dt=F32):
            return ctx.enter_context(nc.sbuf_tensor(name, shape, dt))

        sems = {}

        def sem(name):
            if name not in sems:
                sems[name] = ctx.enter_context(nc.semaphore(name))
            return sems[name]

        bank = ctx.enter_context(nc.psum_tensor("bank", [P, 8, 512], F32))
        full = [sem(f"psum_full{i}") for i in range(8)]
        free = [sem(f"psum_free{i}") for i in range(8)]

        def ps(key, lo=0, hi=512, p0=0, p1=P):
            return bank[p0:p1, use[key][0], lo:hi]

        def claim(pe, key):
            k, n = use[key]
            if n:
                pe.wait_ge(free[k], n)

        def filled(eng, key):
            k, n = use[key]
            eng.wait_ge(full[k], n + 1)

        def read_out(eng, key):
            k, n = use[key]
            eng.wait_ge(free[k], n + 1)

        def full_of(key):
            return full[use[key][0]]

        def free_of(key):
            return free[use[key][0]]

        X = [sb(f"x{i}", [P, B, T]) for i in range(3)]
        dev = sb("dev", [P, B, T])
        sq = sb("sq", [P, 2, T])
        lnv = sb("lnv", [P, 2, T])
        rs = sb("rs", [P, 2, T])
        rs2 = sb("rs2", [P, 2, T])
        nw = sb("nw", [P, 2, T])
        xr = sb("xr", [P, 2, T])
        xm = sb("xm", [P, 2, T])
        X1 = sb("X1", [P, B, T], F32R)
        X2 = sb("X2", [P, B, T], F32R)
        yhi = sb("yhi", [P, 2, 512], F32R)
        Y = sb("Y", [P, B, 2, 512], F32R)
        V0 = sb("V0", [P, B, KT, P])
        V1 = sb("V1", [P, B, KT, H, 32])
        mx = sb("mx", [P, B, H, KT])
        diag = sb("diag", [P, B, H, KT, P], F32R)
        pr = sb("pr", [P, B, H * KT * T])
        rden = sb("rden", [P, 2, T])
        att = sb("att", [P, 2, T])
        ident = sb("ident", [P, P])
        identb = sb("identb", [P, P], BF16)
        cmask = sb("cmask", [P, 2, P], BF16)
        onesf = sb("onesf", [P, 32])
        onesc = sb("onesc", [P, T])
        onesr = sb("onesr", [P, T], F32R)
        avg = sb("avg", [P, P])
        pair = sb("pair", [P, P])
        lows = sb("lows", [P, 3])
        eps = sb("eps", [P, 3])
        half = sb("half", [P, 1])
        iota = sb("iota", [P, E])
        sel = sb("sel", [2 * E, E, 2, C], F32R)
        st6 = sb("st6", [P, B, 6])
        mv = sb("mv", [P, B, 2])
        gmv = sb("gmv", [P, B, 2])
        gt = sb("gt", [P, 6, B])
        grow = sb("grow", [P, C])
        wq0 = sb("wq0", [P, 3, C])
        wg0 = sb("wg0", [P, 3, 2, C])
        m_hi = sb("m_hi", [P, H, P], F32R)
        m_st = sb("m_st", [P, H, P], F32R)
        v_hi = sb("v_hi", [P, P], F32R)
        v_st = sb("v_st", [P, P], F32R)
        wo0 = sb("wo0", [P, P])
        wo0t = sb("wo0t", [P, P])
        bcol = sb("bcol", [P, 2])
        NW = 3 * C + E
        w_raw = sb("w_raw", [P, 2, NW])
        w_hi = sb("w_hi", [P, 2, NW], F32R)
        w_st = sb("w_st", [P, 2, NW], F32R)
        w_qk = sb("w_qk", [P, 2, 2 * H, 4, D1], F32R)
        wo1t = sb("wo1t", [P, 2, C])
        w1_raw = sb("w1_raw", [P, E, F])
        w1_hi = sb("w1_hi", [P, E * F], F32R)
        w1_st = sb("w1_st", [P, E * F], F32R)
        w2_sb = sb("w2_sb", [P, NK, C])
        b1_raw = sb("b1_raw", [NK, P])
        b2_raw = sb("b2_raw", [E, 2, C])
        b1c = sb("b1c", [P, NK])
        b2c = sb("b2c", [P, E])
        lg = sb("lg", [P, TT, E])
        m8 = sb("m8", [P, TT, 8])
        i8 = sb("i8", [P, TT, 8], U32)
        i2 = sb("i2", [P, 2, TT])
        df = sb("df", [P, TT])
        th = sb("th", [P, TT])
        wt = sb("wt", [P, 2, TT])
        eq = sb("eq", [P, 2, TT, E])
        wd = sb("wd", [P, TT // 2, 2, E])
        wT = sb("wT", [2 * E, 2, HALF], F32R)
        hid = sb("hid", [P, 3, 2, HALF])
        ye = sb("ye", [P, 2, HALF])
        yw = sb("yw", [P, 2, HALF])
        acc = sb("acc", [P, HALF])
        res = sb("res", [P, HALF])

        ld = {n: sem("ld_" + n) for n in ("x", "a", "g", "b", "c", "w1", "w2")}
        stored = sem("stored")
        consts = sem("consts")
        cst = sem("cst")
        stats = sem("stats")
        gact = sem("gact")
        prep_v = sem("prep_v")
        prep_g = sem("prep_g")
        prep_a = sem("prep_a")
        S = {(n, l): sem(f"{n}{l}") for l in range(3) for n in
             ("dev", "sq", "lnv", "rs", "rs2", "nw", "xr", "xm", "X1", "X2")}
        S |= {(n, l): sem(f"{n}{l}") for l in range(2) for n in
              ("mx", "diag", "rden", "att", "xout")}
        S |= {n: sem(n) for n in ("yhi",)}
        gsteps = sem("gsteps")
        tanh = sem("tanh")
        wt_hi = sem("wt_hi")
        wt_lo = sem("wt_lo")
        hused = sem("hused")
        summed = sem("summed")
        result = sem("result")

        block = ctx.enter_context(nc.Block())

        def f32(ap):
            return ap.bitcast(F32)

        xo = x.rearrange("b c h w -> c b (h w)")
        oo = out.rearrange("b c h w -> c b (h w)")

        @block.sync
        def _(sp):
            sp.dma_start(X[0][0:C, :, :], xo).then_inc(ld["x"], 16)
            sp.dma_start(X[0][C:P, :, :], xo).then_inc(ld["x"], 16)
            sp.dma_start(wq0[:, :, :], wqkv0.rearrange("(t p) c -> p t c", p=P)).then_inc(ld["a"], 16)
            sp.dma_start(grow[:, :], g0.partition_broadcast(P)).then_inc(ld["a"], 16)
            sp.dma_start(wo0[0:C, :], wout0).then_inc(ld["g"], 16)
            sp.dma_start(wo0[C:P, :], wout0).then_inc(ld["g"], 16)
            for l, b_ in ((0, bout0), (1, bout1)):
                for p0 in (0, C):
                    sp.dma_start(bcol[p0:p0 + C, l:l + 1], b_.rearrange("(c o) -> c o", o=1)).then_inc(ld["b"], 16)
            sp.wait_ge(consts, 1)
            for p0 in (0, C):
                sp.dma_start(w_raw[p0:p0 + C, 0, 0:3 * C], wqkv1).then_inc(ld["c"], 16)
                sp.dma_start(w_raw[p0:p0 + C, 0, 3 * C:NW], wg).then_inc(ld["c"], 16)
                sp.dma_start(w_raw[p0:p0 + 1, 1, 0:3 * C], bqkv1.rearrange("(o c) -> o c", o=1)).then_inc(ld["c"], 16)
                sp.dma_start(w_raw[p0:p0 + 1, 1, 3 * C:NW], bg.rearrange("(o c) -> o c", o=1)).then_inc(ld["c"], 16)
            for h in range(H):
                for r in range(2):
                    sp.dma_start(wo1t[32 * h:32 * h + D1, r, :], wout1[D1 * h:D1 * h + D1, :]).then_inc(ld["b"], 16)
            for p0 in (0, C):
                sp.dma_start(w1_raw[p0:p0 + C, :, :], w1.rearrange("e c f -> c e f")).then_inc(ld["w1"], 16)
            sp.dma_start(w2_sb[:, :, :], w2.rearrange("e (j p) c -> p (e j) c", p=P)).then_inc(ld["w2"], 16)
            sp.dma_start(b1_raw[:, :], b1.rearrange("e (j p) -> (e j) p", p=P)).then_inc(ld["g"], 16)
            for r in range(2):
                sp.dma_start(b2_raw[:, r, :], b2).then_inc(ld["g"], 16)
            sp.wait_ge(result, 1)
            sp.dma_start(oo[:, 0:2, :], res[0:C, :].rearrange("p (b t) -> p b t", b=2)).then_inc(stored, 16)
            sp.wait_ge(stored, 32)

        @block.gpsimd
        def _(pool):
            nc.gpsimd.memset(w_raw[:, :, :], 0.0)
            nc.gpsimd.memset(wo1t[:, :, :], 0.0).then_inc(consts, 1)
            nc.gpsimd.memset(ident[:, :], 0.0).then_inc(consts, 1)
            nc.gpsimd.memset(pair[:, :], 0.5).then_inc(consts, 1)
            nc.gpsimd.memset(cmask[:, :, :], 0.0).then_inc(consts, 1)
            pool.wait_ge(consts, 4)
            nc.gpsimd.affine_select(out=ident[:, :], in_=ident[:, :], compare_op=ALU.not_equal, fill=1.0,
                                    base=0, pattern=[[-1, P]], channel_multiplier=1).then_inc(consts, 1)
            pv = pair[:, :].rearrange("p (g r) -> p g r", r=2)
            nc.gpsimd.affine_select(out=pv, in_=pv, compare_op=ALU.is_ge, fill=0.0, base=0,
                                    pattern=[[-2, C], [0, 2]], channel_multiplier=1).then_inc(consts, 1)
            nc.gpsimd.affine_select(out=cmask[:, 0, :], in_=cmask[:, 0, :], compare_op=ALU.is_ge, fill=MASKED,
                                    base=0, pattern=[[-1, P]], channel_multiplier=1).then_inc(consts, 1)
            nc.gpsimd.affine_select(out=cmask[:, 1, :], in_=cmask[:, 1, :], compare_op=ALU.is_ge, fill=MASKED,
                                    base=0, pattern=[[1, P]], channel_multiplier=-1).then_inc(consts, 1)
            pool.wait_ge(consts, 8)
            nc.gpsimd.affine_select(out=pv, in_=pv, compare_op=ALU.is_ge, fill=0.0, base=1,
                                    pattern=[[2, C], [0, 2]], channel_multiplier=-1).then_inc(consts, 1)
            nc.gpsimd.iota(iota[:, :], pattern=[[1, E]], base=0, channel_multiplier=0,
                           allow_small_or_imprecise_dtypes=True).then_inc(consts, 1)
            nc.gpsimd.memset(V1[:, :, :, :, :], 0.0).then_inc(consts, 1)

            def repeat_qk():
                pool.wait_ge(prep_v, 3)
                src = w_st[:, :, 0:2 * C].rearrange("p s (h d) -> p s h d", d=D1)
                for r in range(4):
                    nc.gpsimd.tensor_copy(w_qk[:, :, :, r, :], f32(src)).then_inc(prep_g, 1)

            raw = w1_raw[:, :, :].rearrange("p e f -> p (e f)")

            def split_w1(i):
                pool.wait_ge(ld["w1"], 32)
                q = E * F // 4
                c = slice(i * q, (i + 1) * q)
                if i == 0:
                    pool.wait_ge(cst, 4)
                nc.gpsimd.tensor_scalar(w1_hi[:, c], raw[:, c], lows[:, 0:1], None, ALU.mult).then_inc(prep_g, 1)
                pool.wait_ge(prep_g, 4 + 2 * i + 1)
                nc.gpsimd.tensor_tensor(w1_st[:, c], raw[:, c], f32(w1_hi[:, c]), ALU.add).then_inc(prep_g, 1)

            def norm(l, b):
                k = b % 2
                if l:
                    read_out(pool, ("mean", l, b))
                pool.wait_ge(S["rs", l], b + 1)
                nc.gpsimd.tensor_tensor(rs2[:, k, :], rs[:, k, :], rs[:, k, :], ALU.mult).then_inc(S["rs2", l], 1)
                nc.gpsimd.tensor_tensor(xr[:, k, :], dev[:, b, :], rs[:, k, :], ALU.mult).then_inc(S["xr", l], 1)

            def maxima(l, b):
                for u in range(4):
                    read_out(pool, (f"s{u}", l, b))
                    if l == 0:
                        which = [(u, 0), (u, 1)]
                    else:
                        which = [(u % 2, u // 2), (u % 2 + 2, u // 2)]
                    for h, q in which:
                        nc.gpsimd.tensor_scalar(diag[:, b, h, q, :], ident[:, :], mx[:, b, h, q:q + 1], -1.0,
                                                ALU.mult, ALU.mult).then_inc(S["diag", l], 1)

            n = 0
            for step, l, b in ORDER:
                if step == "norm":
                    norm(l, b)
                if step == "maxima":
                    maxima(l, b)
                    if (l, b) == (0, 0):
                        repeat_qk()
                if step == "out" and n < 4:
                    split_w1(n)
                    n += 1

            for e in range(E):
                read_out(pool, ("w", e))
                if e == 0:
                    x2 = X[2][:, :, :]
                    nc.gpsimd.tensor_tensor(acc[0:C, :], yw[0:C, 0, :], x2[0:C, 0:2, :].rearrange("p b t -> p (b t)"), ALU.add).then_inc(summed, 1)
                    pool.wait_ge(summed, 1)
                    nc.gpsimd.tensor_tensor(acc[C:P, :], yw[C:P, 0, :], x2[C:P, 2:4, :].rearrange("p b t -> p (b t)"), ALU.add).then_inc(summed, 1)
                elif e < E - 1:
                    pool.wait_ge(summed, e + 1)
                    nc.gpsimd.tensor_tensor(acc[:, :], acc[:, :], yw[:, e % 2, :], ALU.add).then_inc(summed, 1)

        @block.scalar
        def _(act):
            act.wait_ge(stats, 4)
            nc.scalar.activation(gt[:, 3, :], gt[:, 2, :], ACT.Ln).then_inc(gact, 1)
            act.wait_ge(gact, 1)
            nc.scalar.activation(gt[:, 3, :], gt[:, 3, :], ACT.Exp, scale=-0.5).then_inc(gact, 1)
            for h in range(H):
                filled(act, ("prep_m", h))
            nc.scalar.activation(m_hi[:, :, :], bank[:, 0:H, 0:P], ACT.Copy).then_inc(prep_a, 1)
            filled(act, "prep_t")
            nc.scalar.activation(v_hi[:, :], ps("prep_t", 0, P), ACT.Copy).then_inc(prep_a, 1)
            nc.scalar.activation(wo0t[:, :], ps("prep_t", P, 2 * P), ACT.Copy).then_inc(prep_a, 1)
            nc.scalar.activation(b1c[:, :], ps("prep_t", 2 * P, 2 * P + NK), ACT.Copy).then_inc(prep_a, 1)
            nc.scalar.activation(b2c[:, :], ps("prep_t", 3 * P, 3 * P + E), ACT.Copy).then_inc(prep_a, 1)

            def norm(l, b):
                k = b % 2
                n = b
                if l:
                    read_out(act, ("mean", l, b))
                else:
                    act.wait_ge(S["dev", 0], b + 1)
                nc.scalar.activation(sq[:, k, :], dev[:, b, :], ACT.Square).then_inc(S["sq", l], 1)
                filled(act, ("var", l, b))
                nc.scalar.activation(lnv[:, k, :], ps(("var", l, b), 0, T), ACT.Ln, bias=eps[:, l:l + 1]).then_inc(S["lnv", l], 1)
                act.wait_ge(S["lnv", l], b + 1)
                nc.scalar.activation(rs[:, k, :], lnv[:, k, :], ACT.Exp, scale=-0.5).then_inc(S["rs", l], 1)
                act.wait_ge(S["xm", l], b + 1)
                nc.scalar.activation(X1[:, b, :], xm[:, k, :], ACT.Copy, scale=-0.5).then_inc(S["X1", l], 1)

            def project(l, b):
                for u in range(2):
                    key = (f"y{u}", l, b)
                    filled(act, key)
                    if (l, b) in before:
                        read_out(act, (f"y{u}", *before[l, b]))
                    nc.scalar.activation(yhi[:, u, :], ps(key), ACT.Copy).then_inc(S["yhi"], 1)
                key = ("v", l, b)
                filled(act, key)
                if l == 0:
                    nc.scalar.activation(V0[:, b, :, :], ps(key, 0, KT * P).rearrange("p (k c) -> p k c", k=KT),
                                         ACT.Copy).then_inc(free_of(key), 1)
                else:
                    act.wait_ge(consts, 11)
                    for t in range(KT):
                        i = nc.scalar.activation(V1[:, b, t, :, 0:D1],
                                                 ps(key, t * C, t * C + C).rearrange("p (h d) -> p h d", h=H), ACT.Copy)
                    i.then_inc(free_of(key), 1)

            def probs(l, b):
                for u in range(4):
                    key = (f"t{u}", l, b)
                    filled(act, key)
                    c, n = (512 * u, 512) if l == 0 or u < 2 else (512 + T * u, T)
                    nc.scalar.activation(pr[:, b, c:c + n], ps(key, 0, n), ACT.Exp,
                                         scale=SCALE[l]).then_inc(free_of(key), 1)

            for step, l, b in ORDER:
                if step == "norm":
                    norm(l, b)
                if step == "project":
                    project(l, b)
                if step == "probs":
                    probs(l, b)

            def gelus(k):
                filled(act, ("h", k))
                if k >= 3:
                    e, j = divmod(k - 3, FT)
                    if j == FT - 1:
                        filled(act, ("y", e))
                    else:
                        act.wait_ge(hused, e + 1)
                nc.scalar.activation(hid[:, k % 3, :, :], bank[:, 2 * (k % 2):2 * (k % 2) + 2, :], ACT.Gelu,
                                     bias=b1c[:, k:k + 1]).then_inc(free_of(("h", k)), 1)

            def outputs(e):
                filled(act, ("y", e))
                if e >= 2:
                    read_out(act, ("w", e - 2))
                nc.scalar.activation(ye[:, e % 2, :], ps(("y", e)), ACT.Identity, bias=b2c[:, e:e + 1]).then_inc(free_of(("y", e)), 1)

            for k in range(NK):
                gelus(k)
                if k == 0:
                    act.wait_ge(gsteps, 3)
                    nc.scalar.activation(th[:, :], df[:, :], ACT.Tanh, scale=0.5).then_inc(tanh, 1)
                if k == 2:
                    filled(act, "gate_t")
                    nc.scalar.activation(wT[:, 0, :], ps("gate_t", p1=2 * E), ACT.Copy).then_inc(wt_hi, 1)
                if k % FT == 0 and k >= FT:
                    outputs(k // FT - 1)
            outputs(E - 1)
            act.wait_ge(result, 1)
            act.dma_start(oo[:, 2:4, :], res[C:P, :].rearrange("p (b t) -> p b t", b=2)).then_inc(stored, 16)
            act.wait_ge(stored, 32)

        @block.vector
        def _(dve):
            nc.vector.memset(onesf[:, :], 1.0)
            nc.vector.memset(onesc[:, :], 1.0)
            nc.vector.memset(avg[:, :], 1.0 / P)
            for l in range(3):
                nc.vector.memset(eps[:, l:l + 1], EPS[l])
            nc.vector.memset(half[:, :], 0.5).then_inc(cst, 1)
            dve.wait_ge(cst, 1)
            nc.vector.tensor_copy(onesr[:, :], onesc[:, :]).then_inc(cst, 1)
            dve.wait_ge(consts, 5)
            nc.vector.tensor_copy(identb[:, :], ident[:, :]).then_inc(cst, 1)
            nc.vector.tensor_reduce(lows[:, 0:1], ident[:, C:P], AX.X, ALU.add, negate=True)
            nc.vector.tensor_reduce(lows[:, 1:2], ident[:, :].rearrange("p (a r c) -> p a r c", r=2, c=16)[:, :, 1, :],
                                    AX.XY, ALU.add, negate=True)
            nc.vector.tensor_reduce(lows[:, 2:3], ident[:, :].rearrange("p (a r c) -> p a r c", r=2, c=32)[:, :, 1, :],
                                    AX.XY, ALU.add, negate=True).then_inc(cst, 1)
            for e in range(E):
                for s in range(2):
                    i = nc.vector.tensor_copy(sel[:, e, s, :], ident[0:2 * E, E * s + e:E * s + e + 1].to_broadcast([2 * E, C]))
            i.then_inc(cst, 1)

            dve.wait_ge(ld["x"], 32)
            for b in range(B):
                i = nc.vector.bn_stats(st6[:, b, :], X[0][:, b, :])
            i.then_inc(stats, 1)
            dve.wait_ge(stats, 1)
            for b in range(B):
                i = nc.vector.bn_aggr(mv[:, b, :], st6[:, b, :])
            i.then_inc(stats, 1)
            dve.wait_ge(ld["a"], 32)
            for t in range(3):
                for r in range(2):
                    i = nc.vector.tensor_tensor(wg0[:, t, r, :], wq0[:, t, :], grow[:, :], ALU.mult)
            i.then_inc(prep_v, 1)
            filled(dve, "group")
            nc.vector.tensor_copy(gmv[:, :, :], ps("group", 0, 2 * B).rearrange("p (b s) -> p b s", s=2)).then_inc(free_of("group"), 1)
            dve.wait_ge(free_of("group"), 1)
            nc.vector.tensor_tensor(gt[:, 0, :], mv[:, :, 0], gmv[:, :, 0], ALU.subtract).then_inc(stats, 1)
            dve.wait_ge(stats, 3)
            link = sem("group_chain")
            nc.vector.tensor_tensor(gt[:, 1, :], gt[:, 0, :], gt[:, 0, :], ALU.mult).then_inc(link, 1)
            dve.wait_ge(link, 1)
            nc.vector.scalar_tensor_tensor(gt[:, 2, :], gt[:, 1, :], GN_EPS, gmv[:, :, 1], ALU.add, ALU.add).then_inc(stats, 1)
            dve.wait_ge(gact, 2)
            nc.vector.tensor_tensor(gt[:, 4, :], gt[:, 3, :], gt[:, 3, :], ALU.mult).then_inc(link, 1)
            dve.wait_ge(link, 2)
            nc.vector.tensor_tensor(gt[:, 5, :], gt[:, 4, :], gt[:, 2, :], ALU.mult).then_inc(link, 1)
            dve.wait_ge(link, 3)
            nc.vector.tensor_scalar(gt[:, 4, :], gt[:, 5, :], -0.5, 1.5, ALU.mult, ALU.add).then_inc(link, 1)
            dve.wait_ge(link, 4)
            nc.vector.tensor_tensor(gt[:, 0, :], gt[:, 3, :], gt[:, 4, :], ALU.mult).then_inc(link, 1)
            dve.wait_ge(link, 5)
            nc.vector.scalar_tensor_tensor(gt[:, 1, :], gmv[:, :, 0], -1.0, gt[:, 0, :], ALU.mult, ALU.mult).then_inc(link, 1)
            dve.wait_ge(link, 6)

            dve.wait_ge(cst, 4)
            dve.wait_ge(prep_a, 1)
            for h in range(H):
                nc.vector.scalar_tensor_tensor(m_st[:, h, :], f32(m_hi[:, h, :]), lows[:, 0:1],
                                               ps(("prep_m", h), 0, P), ALU.mult, ALU.add).then_inc(free_of(("prep_m", h)), 1)
            dve.wait_ge(prep_a, 5)
            nc.vector.scalar_tensor_tensor(v_st[:, :], f32(v_hi[:, :]), lows[:, 0:1], ps("prep_t", 0, P),
                                           ALU.mult, ALU.add).then_inc(free_of("prep_t"), 1)

            def prep_layer1():
                dve.wait_ge(ld["c"], 8 * 16)
                nc.vector.tensor_copy(w_hi[:, :, :], w_raw[:, :, :]).then_inc(prep_v, 1)
                dve.wait_ge(prep_v, 2)
                nc.vector.scalar_tensor_tensor(w_st[:, :, :], f32(w_hi[:, :, :]), lows[:, 0:1], w_raw[:, :, :],
                                               ALU.mult, ALU.add).then_inc(prep_v, 1)

            def norm(l, b):
                k = b % 2
                if l == 0:
                    nc.vector.tensor_scalar(dev[:, b, :], X[0][:, b, :], gt[:, 0, b:b + 1], gt[:, 1, b:b + 1],
                                            ALU.mult, ALU.add).then_inc(S["dev", 0], 1)
                else:
                    key = ("mean", l, b)
                    filled(dve, key)
                    nc.vector.tensor_tensor(dev[:, b, :], X[l][:, b, :], ps(key, 0, T), ALU.subtract).then_inc(free_of(key), 1)
                dve.wait_ge(S["rs2", l], b + 1)
                nc.vector.scalar_tensor_tensor(nw[:, k, :], ps(("var", l, b), 0, T), EPS[l], rs2[:, k, :],
                                               ALU.add, ALU.mult).then_inc(free_of(("var", l, b)), 1)
                vk, vn = use["var", l, b]
                dve.wait_ge(free[vk], vn + 1)
                dve.wait_ge(S["xr", l], b + 1)
                nc.vector.scalar_tensor_tensor(xm[:, k, :], nw[:, k, :], -3.0, xr[:, k, :], ALU.add, ALU.mult).then_inc(S["xm", l], 1)
                dve.wait_ge(S["X1", l], b + 1)
                nc.vector.scalar_tensor_tensor(X2[:, b, :], xm[:, k, :], -0.5, f32(X1[:, b, :]),
                                               ALU.mult, ALU.subtract).then_inc(S["X2", l], 1)

            def project(l, b):
                for u in range(2):
                    key = (f"y{u}", l, b)
                    dve.wait_ge(S["yhi"], 2 * number[l, b] + u + 1)
                    low = lows[:, 0:1] if l == 0 else lows[:, 1 + u:2 + u]
                    nc.vector.scalar_tensor_tensor(Y[:, b, u, :], f32(yhi[:, u, :]), low, ps(key),
                                                   ALU.mult, ALU.add).then_inc(free_of(key), 1)

            def maxima(l, b):
                for u in range(4):
                    key = (f"s{u}", l, b)
                    filled(dve, key)
                    if l == 0:
                        o, i = mx[:, b, u, :], ps(key).rearrange("p (q t) -> p q t", q=KT)
                    else:
                        q, n = u // 2, P * (u // 2 + 1)
                        o = mx[:, b, :, q].rearrange("p (a r) -> p r a", r=2)[:, u % 2, :]
                        i = ps(key, 0, 2 * n).rearrange("p (h t) -> p h t", h=2)
                    nc.vector.tensor_reduce(o, i, AX.X, ALU.max).then_inc(free_of(key), 1)

            def out_(l, b):
                k = b % 2
                key = ("pv", l, b)
                filled(dve, key)
                nc.vector.reciprocal(rden[:, k, :], ps(key, T, 2 * T)).then_inc(S["rden", l], 1)
                dve.wait_ge(S["rden", l], b + 1)
                nc.vector.tensor_tensor(att[:, k, :], ps(key, 0, T), rden[:, k, :], ALU.mult).then_inc(free_of(key), 1)
                key = ("o", l, b)
                filled(dve, key)
                nc.vector.scalar_tensor_tensor(X[l + 1][:, b, :], ps(key, 0, T), bcol[:, l:l + 1], X[l][:, b, :],
                                               ALU.add, ALU.add).then_inc(free_of(key), 1)

            dve.wait_ge(ld["b"], 16 * (4 + 2 * H))
            first = True
            for step, l, b in ORDER:
                if step == "norm":
                    norm(l, b)
                if step == "project":
                    project(l, b)
                    if first:
                        prep_layer1()
                        first = False
                if step == "maxima":
                    maxima(l, b)
                if step == "out":
                    out_(l, b)

            filled(dve, "gate")
            nc.vector.tensor_copy(lg[:, :, :], ps("gate", 0, TT * E).rearrange("p (t e) -> p t e", e=E)).then_inc(free_of("gate"), 1)
            gk, gn = use["gate"]
            dve.wait_ge(free[gk], gn + 1)
            for t in range(TT):
                i = nc.vector.max(m8[:, t, :], lg[:, t, :])
            i.then_inc(gsteps, 1)
            dve.wait_ge(gsteps, 1)
            for t in range(TT):
                i = nc.vector.max_index(i8[:, t, :], m8[:, t, :], lg[:, t, :])
            i.then_inc(gsteps, 1)
            nc.vector.tensor_tensor(df[:, :], m8[:, :, 0], m8[:, :, 1], ALU.subtract).then_inc(gsteps, 1)
            dve.wait_ge(gsteps, 2)
            for s in range(2):
                i = nc.vector.tensor_copy(i2[:, s, :], i8[:, :, s])
            i.then_inc(gsteps, 1)
            dve.wait_ge(tanh, 1)
            nc.vector.tensor_scalar(wt[:, 0, :], th[:, :], 0.5, 0.5, ALU.mult, ALU.add)
            nc.vector.tensor_scalar(wt[:, 1, :], th[:, :], -0.5, 0.5, ALU.mult, ALU.add).then_inc(gsteps, 1)
            dve.wait_ge(gsteps, 5)
            for s in range(2):
                i = nc.vector.tensor_tensor(eq[:, s, :, :], iota[:, :].rearrange("p (o e) -> p o e", o=1).to_broadcast([P, TT, E]),
                                            i2[:, s, :].rearrange("p (t o) -> p t o", o=1).to_broadcast([P, TT, E]), ALU.is_equal)
            i.then_inc(gsteps, 1)
            dve.wait_ge(gsteps, 6)
            for s in range(2):
                i = nc.vector.tensor_tensor(eq[:, s, :, :], eq[:, s, :, :],
                                            wt[:, s, :].rearrange("p (t o) -> p t o", o=1).to_broadcast([P, TT, E]), ALU.mult)
            i.then_inc(gsteps, 1)
            dve.wait_ge(gsteps, 7)
            ev = eq[:, :, :, :].rearrange("p s (a j) e -> p s a j e", a=2)
            for a in range(2):
                i = nc.vector.tensor_tensor(wd[:, :, a, :], ev[:, 0, a, :, :], ev[:, 1, a, :, :], ALU.add)
            i.then_inc(gsteps, 1)
            dve.wait_ge(wt_hi, 1)
            nc.vector.tensor_tensor(wT[:, 1, :], ps("gate_t", p1=2 * E), f32(wT[:, 0, :]), ALU.subtract).then_inc(free_of("gate_t"), 1)

            for e in range(E):
                read_out(dve, ("y", e))
                filled(dve, ("w", e))
                if e >= 2:
                    dve.wait_ge(summed, e)
                nc.vector.tensor_tensor(yw[:, e % 2, :], ye[:, e % 2, :], ps(("w", e)), ALU.mult).then_inc(free_of(("w", e)), 1)
            dve.wait_ge(summed, E)
            read_out(dve, ("w", E - 1))
            nc.vector.tensor_tensor(res[:, :], acc[:, :], yw[:, (E - 1) % 2, :], ALU.add).then_inc(result, 1)

        @block.tensor
        def _(pe):
            mm = nc.tensor.matmul
            pe.wait_ge(consts, 9)
            pe.wait_ge(stats, 2)
            mm(ps("group", 0, 2 * B), pair[:, :], mv[:, :, :].rearrange("p b s -> p (b s)"), start=True, stop=True).then_inc(full_of("group"), 1)
            pe.wait_ge(prep_v, 1)
            for h in range(H):
                mm(ps(("prep_m", h), 0, P), wg0[D0 * h:D0 * h + D0, 0, :, :].rearrange("p r c -> p (r c)"),
                       wg0[D0 * h:D0 * h + D0, 1, :, :].rearrange("p r c -> p (r c)"), start=True,
                   stop=True).then_inc(full_of(("prep_m", h)), 1)
            pe.wait_ge(ld["g"], 16 * 5)
            nc.tensor.transpose(ps("prep_t", 0, P), wg0[:, 2, :, :].rearrange("p r c -> p (r c)"), ident[:, :])
            nc.tensor.transpose(ps("prep_t", P, 2 * P), wo0[:, :], ident[:, :])
            nc.tensor.transpose(ps("prep_t", 2 * P, 2 * P + NK), b1_raw[:, :], ident[0:NK, 0:NK])
            nc.tensor.transpose(ps("prep_t", 3 * P, 3 * P + E), b2_raw[:, :, :].rearrange("p r c -> p (r c)"),
                                ident[0:E, 0:E]).then_inc(full_of("prep_t"), 1)

            def norm(l, b):
                if l:
                    key = ("mean", l, b)
                    claim(pe, key)
                    read_out(pe, ("o", l - 1, b))
                    mm(ps(key, 0, T), avg[:, :], X[l][:, b, :], start=True, stop=True).then_inc(full_of(key), 1)
                key = ("var", l, b)
                claim(pe, key)
                pe.wait_ge(S["sq", l], b + 1)
                mm(ps(key, 0, T), avg[:, :], sq[:, b % 2, :], start=True, stop=True).then_inc(full_of(key), 1)

            def project(l, b):
                pe.wait_ge(S["X1", l], b + 1)
                pe.wait_ge(S["X2", l], b + 1)
                for u in range(2):
                    key = (f"y{u}", l, b)
                    claim(pe, key)
                    if b == 0 and l == 0:
                        for v in range(2):
                            pe.wait_ge(free_of(("prep_m", 2 * u + v)), 1)
                    elif b == 0:
                        pe.wait_ge(prep_g, 4)
                    for v in range(2):
                        o = ps(key, T * v, T * v + T)
                        if l == 0:
                            w = m_st[:, 2 * u + v, :]
                            mm(o, w, X1[:, b, :], start=True, stop=False)
                            i = mm(o, w, X2[:, b, :], start=False, stop=True)
                        else:
                            heads = slice(H * u + 2 * v, H * u + 2 * v + 2)
                            w, bias = (w_qk[:, s, heads, :, :].rearrange("p h r d -> p (h r d)") for s in range(2))
                            mm(o, w, X1[:, b, :], start=True, stop=False)
                            mm(o, w, X2[:, b, :], start=False, stop=False)
                            i = mm(o, bias, onesr[:, :], start=False, stop=True)
                    i.then_inc(full_of(key), 1)
                key = ("v", l, b)
                claim(pe, key)
                if l == 0 and b == 0:
                    pe.wait_ge(free_of("prep_t"), 1)
                for t in range(KT):
                    tok = slice(P * t, P * t + P)
                    if l == 0:
                        o = ps(key, P * t, P * t + P)
                        mm(o, X1[:, b, tok], v_st[:, :], start=True, stop=False)
                        i = mm(o, X2[:, b, tok], v_st[:, :], start=False, stop=True)
                    else:
                        o = ps(key, C * t, C * t + C)
                        mm(o, X1[:, b, tok], w_st[:, 0, 2 * C:3 * C], start=True, stop=False)
                        mm(o, X2[:, b, tok], w_st[:, 0, 2 * C:3 * C], start=False, stop=False)
                        i = mm(o, onesr[:, 0:P], w_st[:, 1, 2 * C:3 * C], start=False, stop=True)
                i.then_inc(full_of(key), 1)

            def q1(b, h, t0, t1):
                p = C * (h % 2)
                return Y[p:p + C, b, 0, T * (h // 2) + t0:T * (h // 2) + t1]

            def k1(b, h, t0, t1):
                p = C * (h % 2)
                return Y[p:p + C, b, 1, T * (h // 2) + t0:T * (h // 2) + t1]

            def maxima(l, b):
                if l == 0:
                    for h in range(H):
                        key = (f"s{h}", l, b)
                        claim(pe, key)
                        if h % 2 == 0:
                            read_out(pe, (f"y{h // 2}", l, b))
                        for q in range(KT):
                            c = T * (h % 2) + P * q
                            i = mm(ps(key, T * q, T * q + T), Y[:, b, h // 2, c:c + P], X1[:, b, :], start=True, stop=True)
                        i.then_inc(full_of(key), 1)
                    return
                read_out(pe, ("y0", l, b))
                read_out(pe, ("y1", l, b))
                for u in range(4):
                    key = (f"s{u}", l, b)
                    claim(pe, key)
                    q, n = u // 2, P * (u // 2 + 1)
                    for v in range(2):
                        h = u % 2 + 2 * v
                        mm(ps(key, n * v, n * v + n), q1(b, h, P * q, P * q + P), k1(b, h, 0, n), start=True, stop=False)
                        i = mm(ps(key, n * v + n - P, n * v + n), identb[:, :], cmask[:, 0, :], start=False, stop=True)
                    i.then_inc(full_of(key), 1)

            def probs(l, b):
                if l == 0:
                    for h in range(H):
                        key = (f"t{h}", l, b)
                        claim(pe, key)
                        pe.wait_ge(S["diag", l], 8 * b + 2 * h + 2)
                        y = Y[:, b, h // 2, T * (h % 2):T * (h % 2) + T]
                        for t in range(KT):
                            tok = slice(P * t, P * t + P)
                            o = ps(key, T * t, T * t + T)
                            mm(o, X1[:, b, tok], y, start=True, stop=False)
                            mm(o, X2[:, b, tok], y, start=False, stop=False)
                            i = mm(o, onesr[:, 0:P], diag[:, b, h, :, :].rearrange("p q c -> p (q c)"), start=False, stop=True)
                        i.then_inc(full_of(key), 1)
                    return
                for u in range(4):
                    key = (f"t{u}", l, b)
                    claim(pe, key)
                    pe.wait_ge(S["diag", l], 8 * b + (6, 8, 8, 8)[u])
                    k0 = P * (u // 2)
                    n = T - k0
                    for v in range(2):
                        h = u % 2 + 2 * v
                        o = ps(key, n * v, n * v + n)
                        mm(o, k1(b, h, k0, k0 + P), q1(b, h, k0, T), start=True, stop=False)
                        mm(ps(key, n * v, n * v + P), identb[:, :], cmask[:, 1, :], start=False, stop=False)
                        i = mm(o, onesr[:, 0:P], diag[:, b, h, u // 2:KT, :].rearrange("p q c -> p (q c)"), start=False, stop=True)
                    i.then_inc(full_of(key), 1)

            def out_(l, b):
                for u in range(4):
                    read_out(pe, (f"t{u}", l, b))
                read_out(pe, ("v", l, b))
                key = ("pv", l, b)
                claim(pe, key)
                for den in range(2):
                    for t in range(KT):
                        for h in range(H):
                            if l == 0:
                                w, p, q0 = V0[:, b, t, D0 * h:D0 * h + D0], pr[:, b, 512 * h + T * t:512 * h + T * t + T], 0
                            elif t == 0:
                                c = 512 * (h % 2) + T * (h // 2)
                                w, p, q0 = V1[:, b, t, h, :], pr[:, b, c:c + T], 0
                            else:
                                c = 1024 + T * (h % 2) + P * (h // 2)
                                w, p, q0 = V1[:, b, t, h, :], pr[:, b, c:c + P], P
                            if den:
                                w = onesf[:, :]
                            i = mm(ps(key, T * den + q0, T * den + T, 32 * h, 32 * h + 32), w, p,
                                   start=(t == 0), stop=(t == KT - 1))
                i.then_inc(full_of(key), 1)
                key = ("o", l, b)
                claim(pe, key)
                if b == 0 and l == 1:
                    pe.wait_ge(ld["b"], 16 * (4 + 2 * H))
                read_out(pe, ("pv", l, b))
                w = wo0t[:, :] if l == 0 else wo1t[:, :, :].rearrange("p r c -> p (r c)")
                mm(ps(key, 0, T), w, att[:, b % 2, :], start=True, stop=True).then_inc(full_of(key), 1)

            run = {"norm": norm, "project": project, "maxima": maxima, "probs": probs, "out": out_}
            for step, l, b in ORDER:
                run[step](l, b)

            pe.wait_ge(S["X2", 2], B)
            pe.wait_ge(prep_g, 12)

            def up(k):
                key = ("h", k)
                claim(pe, key)
                if k < 2:
                    pe.wait_ge(free[use[key][0] + 1], ring_used[use[key][0] + 1])
                for s in range(2):
                    w = w1_st[:, P * k:P * k + P]
                    o = bank[:, use[key][0] + s, :]
                    x1, x2 = (G[:, 2 * s:2 * s + 2, :].rearrange("p b t -> p (b t)") for G in (X1, X2))
                    mm(o, w, x1, start=True, stop=False)
                    i = mm(o, w, x2, start=False, stop=True)
                i.then_inc(full_of(key), 1)

            def down(k):
                e, j = divmod(k, FT)
                key = ("y", e)
                if j == 0:
                    claim(pe, key)
                read_out(pe, ("h", k))
                for s in range(2):
                    i = mm(ps(key, p0=C * s, p1=C * s + C), w2_sb[:, k, :], hid[:, k % 3, s, :],
                           start=(j == 0), stop=(j == FT - 1))
                i.then_inc(*((full_of(key), 1) if j == FT - 1 else (hused, 1)))

            def spread(e):
                key = ("w", e)
                claim(pe, key)
                if e == 0:
                    pe.wait_ge(free_of("gate_t"), use["gate_t"][1] + 1)
                w = sel[:, e, :, :].rearrange("p s c -> p (s c)")
                mm(ps(key), w, wT[:, 0, :], start=True, stop=False)
                mm(ps(key), w, wT[:, 1, :], start=False, stop=True).then_inc(full_of(key), 1)

            up(0)
            claim(pe, "gate")
            for t in range(TT):
                b, tok = t // KT, slice(P * (t % KT), P * (t % KT) + P)
                o = ps("gate", E * t, E * t + E)
                mm(o, X1[:, b, tok], w_st[:, 0, 3 * C:NW], start=True, stop=False)
                mm(o, X2[:, b, tok], w_st[:, 0, 3 * C:NW], start=False, stop=False)
                i = mm(o, onesr[:, 0:P], w_st[:, 1, 3 * C:NW], start=False, stop=True)
            i.then_inc(full_of("gate"), 1)
            pe.wait_ge(ld["w2"], 16)
            for k in range(NK):
                if k + 1 < NK:
                    up(k + 1)
                if k == 1:
                    claim(pe, "gate_t")
                    pe.wait_ge(gsteps, 8)
                    for j in range(TT // 2):
                        i = nc.tensor.transpose(ps("gate_t", P * j, P * j + P, p1=2 * E),
                                                wd[:, j, :, :].rearrange("p s e -> p (s e)"), ident[:, :])
                    i.then_inc(full_of("gate_t"), 1)
                down(k)
                if k >= 3 and k % 2 == 1:
                    spread((k - 3) // 2)
            spread(E - 1)


_INS = ['x', 'L0_conv_g', 'L0_conv_w_qkv', 'L0_conv_w_out', 'L0_conv_b_out', 'L1_attn_W_qkv', 'L1_attn_b_qkv',
        'L1_attn_W_out', 'L1_attn_b_out', 'L1_ffn_Wg', 'L1_ffn_bg', 'L1_ffn_W1', 'L1_ffn_b1', 'L1_ffn_W2', 'L1_ffn_b2']
_OUTS = [((4, 64, 16, 16), 'float32')]


def kernel(**inputs):
    import numpy as _np
    import concourse.bacc as _bacc
    from concourse import mybir as _mybir
    from concourse.bass_utils import run_bass_kernel_spmd as _run

    nc = _bacc.Bacc("TRN2", target_bir_lowering=False, num_devices=1)
    arrays, args = {}, []
    for name in _INS:
        a = _np.ascontiguousarray(inputs[name])
        arrays[f"in_{name}_dram"] = a
        args.append(nc.dram_tensor(f"in_{name}_dram", a.shape, _mybir.dt.from_np(a.dtype), kind="ExternalInput").ap())
    for i, (shape, dtype) in enumerate(_OUTS):
        dt = _mybir.dt.from_np(_np.dtype(dtype))
        args.append(nc.dram_tensor(f"out_{i}_dram", shape, dt, kind="ExternalOutput").ap())
    hybrid_block(nc, *args)
    r = _run(nc, [arrays], core_ids=[0])
    return r.results[0]["out_0_dram"]
```

```python
from contextlib import ExitStack

import concourse.bass as bass
from concourse import mybir

F32 = mybir.dt.float32
F32R = mybir.dt.float32r
BF16 = mybir.dt.bfloat16
U32 = mybir.dt.uint32
ALU = mybir.AluOpType
ACT = mybir.ActivationFunctionType
AX = mybir.AxisListType

P = 128
MASKED = -1e30
OFFSETS = (0,1,1,2)


RANK = dict(newton=0, split=0, residual=0, values=0, probs=0, maxima=0, project=0, center=0, scale=0, gate=0)
SMALL = 0


def schedule(offsets):
    norm = ("center", "scale", "newton", "split")
    attention = ("project", "maxima", "probs", "values", "residual")
    chain = [(step, layer) for layer in (0, 1) for step in norm + attention] + [(step, 2) for step in norm + ("gate",)]
    order = []
    for t in range(len(chain) + max(offsets)):
        slot = [(*chain[t - offset], b) for b, offset in enumerate(offsets) if 0 <= t - offset < len(chain)]
        order += sorted(slot, key=lambda entry: RANK[entry[0]])
    return order


def hybrid_block(nc, x, g0, wqkv0, wout0, bout0, wqkv1, bqkv1, wout1, bout1, wg, bg, w1, b1, w2, b2, out):
    B, C, HH, WW = x.shape
    T = HH * WW
    H = 4
    D0 = wqkv0.shape[0] // 3 // H
    D1 = wqkv1.shape[1] // 3 // H
    E, _, F = w1.shape
    KT = T // P
    HP = H // 2
    FT = F // P
    NK = E * FT
    TT = B * T // P
    HALF = B * T // 2
    assert (B, C, T, H, D0, D1, E, F) == (4, 64, 256, 4, 32, 16, 8, 256)
    SCALE = (float(D0) ** -0.5, float(D1) ** -0.5)
    EPS = (1e-12, 1e-5, 1e-5)
    GN_EPS = 1e-5
    ORDER = schedule(OFFSETS)

    use, used = {}, [0] * 8

    def take(key, bank):
        use[key] = (bank, used[bank])
        used[bank] += 1

    for h in range(H):
        take(("prep_m", h), h)
    take("prep_t", 4)
    take("group", 5)
    turn = {True: 0, False: 0}
    for step, layer, b in ORDER:
        names = {
            "center": ["mean"] if layer else [],
            "scale": ["var"],
            "newton": [],
            "split": [],
            "project": ["y0", "y1", "v"],
            "maxima": ["s0", "s1", "s2", "s3"],
            "probs": ["t0", "t1", "t2", "t3"],
            "values": ["pv"],
            "residual": ["o"],
            "gate": ["logits"],
        }[step]
        for name in names:
            small = name in ("mean", "var", "pv", "o", "logits")
            if SMALL == 0:
                small = False
            take((name, layer, b), 8 - SMALL + turn[small] % SMALL if small else turn[small] % (8 - SMALL))
            turn[small] += 1
    ring_used = list(used)
    for k in range(NK):
        take(("h", k), 2 * (k % 2))
    take("gate_t", 7)
    for e in range(E):
        take(("y", e), 4 + e % 2)
        take(("w", e), 6 + e % 2)

    projections = [(l, b) for step, l, b in ORDER if step == "project"]
    number = {key: n for n, key in enumerate(projections)}
    before = dict(zip(projections[1:], projections))

    with ExitStack() as ctx:
        def sb(name, shape, dt=F32):
            return ctx.enter_context(nc.sbuf_tensor(name, shape, dt))

        sems = {}

        def sem(name):
            if name not in sems:
                sems[name] = ctx.enter_context(nc.semaphore(name))
            return sems[name]

        bank = ctx.enter_context(nc.psum_tensor("bank", [P, 8, 512], F32))
        full = [sem(f"psum_full{i}") for i in range(8)]
        free = [sem(f"psum_free{i}") for i in range(8)]

        def ps(key, lo=0, hi=512, p0=0, p1=P):
            return bank[p0:p1, use[key][0], lo:hi]

        def claim(pe, key):
            k, n = use[key]
            if n:
                pe.wait_ge(free[k], n)

        def filled(eng, key):
            k, n = use[key]
            eng.wait_ge(full[k], n + 1)

        def read_out(eng, key):
            k, n = use[key]
            eng.wait_ge(free[k], n + 1)

        def full_of(key):
            return full[use[key][0]]

        def free_of(key):
            return free[use[key][0]]

        X = sb("x", [P, B, T])
        dev = sb("dev", [P, B, T])
        sq = sb("sq", [P, B, T])
        rs2 = sb("rs2", [P, B, T])
        xm = sb("xm", [P, B, T])
        X1 = sb("X1", [P, B, T], F32R)
        X2 = sb("X2", [P, B, T], F32R)
        yhi = sb("yhi", [P, 2, 512], F32R)
        Y = sb("Y", [P, B, 2, 512], F32R)
        V0 = sb("V0", [P, B, KT, P])
        V1 = sb("V1", [P, B, KT, H, 32])
        mx = sb("mx", [P, B, H, KT])
        diag = sb("diag", [P, B, H, KT, P], F32R)
        pr = sb("pr", [P, B, H * KT * T])
        rden = sb("rden", [P, B, T])
        dr = sb("dr", [P, B, T])
        att = sb("att", [P, B, T])
        ident = sb("ident", [P, P])
        identb = sb("identb", [P, P], BF16)
        cmask = sb("cmask", [P, 2, P], BF16)
        onesf = sb("onesf", [P, 32])
        onesc = sb("onesc", [P, T])
        onesr = sb("onesr", [P, T], F32R)
        avg = sb("avg", [P, P])
        pair = sb("pair", [P, P])
        lows = sb("lows", [P, 3])
        eps = sb("eps", [P, 3])
        half = sb("half", [P, 1])
        iota = sb("iota", [P, E])
        sel = sb("sel", [2 * E, E, 2, C], F32R)
        st6 = sb("st6", [P, B, 6])
        mv = sb("mv", [P, B, 2])
        gmv = sb("gmv", [P, B, 2])
        gt = sb("gt", [P, 6, B])
        grow = sb("grow", [P, C])
        wq0 = sb("wq0", [P, 3, C])
        wg0 = sb("wg0", [P, 3, 2, C])
        m_hi = sb("m_hi", [P, H, P], F32R)
        m_st = sb("m_st", [P, H, P], F32R)
        v_hi = sb("v_hi", [P, P], F32R)
        v_st = sb("v_st", [P, P], F32R)
        wo0 = sb("wo0", [P, P])
        wo0t = sb("wo0t", [P, P])
        bcol = sb("bcol", [P, 2])
        NW = 3 * C + E
        w_raw = sb("w_raw", [P, 2, NW])
        w_hi = sb("w_hi", [P, 2, NW], F32R)
        w_st = sb("w_st", [P, 2, NW], F32R)
        w_qk = sb("w_qk", [P, 2, 2 * H, 4, D1], F32R)
        wo1t = sb("wo1t", [P, 2, C])
        w1_raw = sb("w1_raw", [P, E, F])
        w1_hi = sb("w1_hi", [P, E * F // 4], F32R)
        w1_st = sb("w1_st", [P, E * F], F32R)
        w2_sb = sb("w2_sb", [P, NK, C])
        b1_raw = sb("b1_raw", [NK, P])
        b2_raw = sb("b2_raw", [E, 2, C])
        b1c = sb("b1c", [P, NK])
        b2c = sb("b2c", [P, E])
        bgate = sb("bgate", [P, E])
        lg = sb("lg", [P, TT, E])
        m8 = sb("m8", [P, TT, 8])
        i8 = sb("i8", [P, TT, 8], U32)
        i2 = sb("i2", [P, 2, TT])
        df = sb("df", [P, TT])
        th = sb("th", [P, TT])
        wt = sb("wt", [P, 2, TT])
        eq = sb("eq", [P, 2, TT, E])
        wd = sb("wd", [P, TT // 2, 2, E])
        wT = sb("wT", [2 * E, 2, HALF], F32R)
        hid = sb("hid", [P, 3, 2, HALF])
        ye = sb("ye", [P, 2, HALF])
        yw = sb("yw", [P, 2, HALF])
        acc = sb("acc", [P, HALF])

        ld = {n: sem("ld_" + n) for n in ("x", "a", "g", "b", "c", "w1", "w2")}
        stored = sem("stored")
        consts = sem("consts")
        cst = sem("cst")
        stats = sem("stats")
        gact = sem("gact")
        prep_v = sem("prep_v")
        prep_g = sem("prep_g")
        prep_a = sem("prep_a")
        S = {(n, l): sem(f"{n}{l}") for l in range(3) for n in
             ("dev", "sq", "lnv", "r0", "rs2", "xr", "xm", "X1", "X2")}
        S |= {(n, l): sem(f"{n}{l}") for l in range(2) for n in
              ("diag", "lden", "rden", "dr", "att")}
        S |= {n: sem(n) for n in ("yhi",)}
        gsteps = sem("gsteps")
        tanh = sem("tanh")
        wt_hi = sem("wt_hi")
        wt_lo = sem("wt_lo")
        hused = sem("hused")
        summed = sem("summed")
        result = sem("result")

        block = ctx.enter_context(nc.Block())

        def f32(ap):
            return ap.bitcast(F32)

        xo = x.rearrange("b c h w -> c b (h w)")
        oo = out.rearrange("b c h w -> c b (h w)")

        @block.sync
        def _(sp):
            sp.dma_start(X[0:C, :, :], xo).then_inc(ld["x"], 16)
            sp.dma_start(wo0[0:C, :], wout0).then_inc(ld["g"], 16)
            sp.dma_start(wo0[C:P, :], wout0).then_inc(ld["g"], 16)
            sp.dma_start(b1_raw[:, :], b1.rearrange("e (j p) -> (e j) p", p=P)).then_inc(ld["g"], 16)
            for r in range(2):
                sp.dma_start(b2_raw[:, r, :], b2).then_inc(ld["g"], 16)
            sp.wait_ge(consts, 2)
            for p0 in (0, C):
                sp.dma_start(w_raw[p0:p0 + C, 0, 0:3 * C], wqkv1).then_inc(ld["c"], 16)
                sp.dma_start(w_raw[p0:p0 + C, 0, 3 * C:NW], wg).then_inc(ld["c"], 16)
                sp.dma_start(w_raw[p0:p0 + 1, 1, 0:3 * C], bqkv1.rearrange("(o c) -> o c", o=1)).then_inc(ld["c"], 16)
            sp.dma_start(bgate[:, :], bg.partition_broadcast(P)).then_inc(ld["c"], 16)
            for l, b_ in ((0, bout0), (1, bout1)):
                for p0 in (0, C):
                    sp.dma_start(bcol[p0:p0 + C, l:l + 1], b_.rearrange("(c o) -> c o", o=1)).then_inc(ld["b"], 16)
            for h in range(H):
                for r in range(2):
                    sp.dma_start(wo1t[32 * h:32 * h + D1, r, :], wout1[D1 * h:D1 * h + D1, :]).then_inc(ld["b"], 16)
            for p0 in (0, C):
                sp.dma_start(w1_raw[p0:p0 + C, :, :], w1.rearrange("e c f -> c e f")).then_inc(ld["w1"], 16)
            sp.dma_start(w2_sb[:, :, :], w2.rearrange("e (j p) c -> p (e j) c", p=P)).then_inc(ld["w2"], 16)
            sp.wait_ge(result, 1)
            sp.dma_start(oo[:, 0:2, :], acc[0:C, :].rearrange("p (b t) -> p b t", b=2)).then_inc(stored, 16)
            sp.wait_ge(stored, 32)

        @block.gpsimd
        def _(pool):
            nc.gpsimd.memset(w_raw[:, :, :], 0.0).then_inc(consts, 1)
            nc.gpsimd.memset(wo1t[:, :, :], 0.0).then_inc(consts, 1)
            nc.gpsimd.memset(ident[:, :], 0.0).then_inc(consts, 1)
            nc.gpsimd.memset(pair[:, :], 0.5).then_inc(consts, 1)
            nc.gpsimd.memset(cmask[:, :, :], 0.0).then_inc(consts, 1)
            pool.wait_ge(consts, 5)
            nc.gpsimd.affine_select(out=ident[:, :], in_=ident[:, :], compare_op=ALU.not_equal, fill=1.0,
                                    base=0, pattern=[[-1, P]], channel_multiplier=1).then_inc(consts, 1)
            pv = pair[:, :].rearrange("p (g r) -> p g r", r=2)
            nc.gpsimd.affine_select(out=pv, in_=pv, compare_op=ALU.is_ge, fill=0.0, base=0,
                                    pattern=[[-2, C], [0, 2]], channel_multiplier=1).then_inc(consts, 1)
            nc.gpsimd.affine_select(out=cmask[:, 0, :], in_=cmask[:, 0, :], compare_op=ALU.is_ge, fill=MASKED,
                                    base=0, pattern=[[-1, P]], channel_multiplier=1).then_inc(consts, 1)
            nc.gpsimd.affine_select(out=cmask[:, 1, :], in_=cmask[:, 1, :], compare_op=ALU.is_ge, fill=MASKED,
                                    base=0, pattern=[[1, P]], channel_multiplier=-1).then_inc(consts, 1)
            pool.wait_ge(consts, 7)
            nc.gpsimd.affine_select(out=pv, in_=pv, compare_op=ALU.is_ge, fill=0.0, base=1,
                                    pattern=[[2, C], [0, 2]], channel_multiplier=-1).then_inc(consts, 1)
            nc.gpsimd.iota(iota[:, :], pattern=[[1, E]], base=0, channel_multiplier=0,
                           allow_small_or_imprecise_dtypes=True).then_inc(consts, 1)
            nc.gpsimd.memset(V1[:, :, :, :, :], 0.0).then_inc(consts, 1)

            def repeat_qk():
                pool.wait_ge(prep_v, 3)
                src = w_st[:, :, 0:2 * C].rearrange("p s (h d) -> p s h d", d=D1)
                for r in range(4):
                    nc.gpsimd.tensor_copy(w_qk[:, :, :, r, :], f32(src)).then_inc(prep_g, 1)

            raw = w1_raw[:, :, :].rearrange("p e f -> p (e f)")

            def split_w1(i):
                pool.wait_ge(ld["w1"], 32)
                q = E * F // 4
                c = slice(i * q, (i + 1) * q)
                if i == 0:
                    pool.wait_ge(cst, 4)
                else:
                    pool.wait_ge(prep_g, 4 + 2 * i)
                nc.gpsimd.tensor_scalar(w1_hi[:, :], raw[:, c], lows[:, 0:1], None, ALU.mult).then_inc(prep_g, 1)
                pool.wait_ge(prep_g, 4 + 2 * i + 1)
                nc.gpsimd.tensor_tensor(w1_st[:, c], raw[:, c], f32(w1_hi[:, :]), ALU.add).then_inc(prep_g, 1)

            def scale(l, b):
                if l:
                    read_out(pool, ("mean", l, b))
                pool.wait_ge(S["r0", l], b + 1)
                nc.gpsimd.tensor_tensor(xm[:, b, :], dev[:, b, :], sq[:, b, :], ALU.mult).then_inc(S["xr", l], 1)

            def maxima(l, b):
                for u in range(4):
                    read_out(pool, (f"s{u}", l, b))
                    if l == 0:
                        which = [(u, 0), (u, 1)]
                    else:
                        which = [(u % 2, u // 2), (u % 2 + 2, u // 2)]
                    for h, q in which:
                        nc.gpsimd.tensor_scalar(diag[:, b, h, q, :], ident[:, :], mx[:, b, h, q:q + 1], -1.0,
                                                ALU.mult, ALU.mult).then_inc(S["diag", l], 1)

            n = 0
            for step, l, b in ORDER:
                if step == "scale":
                    scale(l, b)
                if step == "maxima":
                    maxima(l, b)
                    if (l, b) == (0, 0):
                        repeat_qk()
                if step == "residual" and n < 4:
                    split_w1(n)
                    n += 1

            for e in range(E):
                read_out(pool, ("w", e))
                if e == 0:
                    x2 = X[:, :, :]
                    nc.gpsimd.tensor_tensor(acc[0:C, :], yw[0:C, 0, :], x2[0:C, 0:2, :].rearrange("p b t -> p (b t)"), ALU.add).then_inc(summed, 1)
                    pool.wait_ge(summed, 1)
                    nc.gpsimd.tensor_tensor(acc[C:P, :], yw[C:P, 0, :], x2[C:P, 2:4, :].rearrange("p b t -> p (b t)"), ALU.add).then_inc(summed, 1)
                elif e < E - 1:
                    pool.wait_ge(summed, e + 1)
                    nc.gpsimd.tensor_tensor(acc[:, :], acc[:, :], yw[:, e % 2, :], ALU.add).then_inc(summed, 1)

        @block.scalar
        def _(act):
            act.dma_start(X[C:P, :, :], xo).then_inc(ld["x"], 16)
            act.dma_start(wq0[:, :, :], wqkv0.rearrange("(t p) c -> p t c", p=P)).then_inc(ld["a"], 16)
            act.dma_start(grow[:, :], g0.partition_broadcast(P)).then_inc(ld["a"], 16)
            nc.scalar.preload_act_table_set("natural_log_exp_and_others")
            act.wait_ge(stats, 4)
            nc.scalar.activation(gt[:, 3, :], gt[:, 2, :], ACT.Ln).then_inc(gact, 1)
            act.wait_ge(gact, 1)
            nc.scalar.activation(gt[:, 3, :], gt[:, 3, :], ACT.Exp, scale=-0.5).then_inc(gact, 1)
            for h in range(H):
                filled(act, ("prep_m", h))
            nc.scalar.activation(m_hi[:, :, :], bank[:, 0:H, 0:P], ACT.Copy).then_inc(prep_a, 1)
            filled(act, "prep_t")
            nc.scalar.activation(v_hi[:, :], ps("prep_t", 0, P), ACT.Copy).then_inc(prep_a, 1)
            nc.scalar.activation(wo0t[:, :], ps("prep_t", P, 2 * P), ACT.Copy).then_inc(prep_a, 1)
            nc.scalar.activation(b1c[:, :], ps("prep_t", 2 * P, 2 * P + NK), ACT.Copy).then_inc(prep_a, 1)
            nc.scalar.activation(b2c[:, :], ps("prep_t", 3 * P, 3 * P + E), ACT.Copy).then_inc(prep_a, 1)

            def center(l, b):
                if l:
                    read_out(act, ("mean", l, b))
                else:
                    act.wait_ge(S["dev", 0], b + 1)
                nc.scalar.activation(sq[:, b, :], dev[:, b, :], ACT.Square).then_inc(S["sq", l], 1)

            def scale(l, b):
                key = ("var", l, b)
                filled(act, key)
                nc.scalar.activation(sq[:, b, :], ps(key, 0, T), ACT.Ln, bias=eps[:, l:l + 1]).then_inc(S["lnv", l], 1)
                act.wait_ge(S["lnv", l], b + 1)
                nc.scalar.activation(sq[:, b, :], sq[:, b, :], ACT.Exp, scale=-0.5).then_inc(S["r0", l], 1)
                act.wait_ge(S["r0", l], b + 1)
                nc.scalar.activation(rs2[:, b, :], sq[:, b, :], ACT.Square).then_inc(S["rs2", l], 1)

            def newton(l, b):
                act.wait_ge(S["xm", l], b + 1)
                nc.scalar.activation(X1[:, b, :], xm[:, b, :], ACT.Copy, scale=-0.5).then_inc(S["X1", l], 1)

            def project(l, b):
                for u in range(2):
                    key = (f"y{u}", l, b)
                    filled(act, key)
                    if (l, b) in before:
                        read_out(act, (f"y{u}", *before[l, b]))
                    nc.scalar.activation(yhi[:, u, :], ps(key), ACT.Copy).then_inc(S["yhi"], 1)
                key = ("v", l, b)
                filled(act, key)
                if l == 0:
                    nc.scalar.activation(V0[:, b, :, :], ps(key, 0, KT * P).rearrange("p (k c) -> p k c", k=KT),
                                         ACT.Copy).then_inc(free_of(key), 1)
                else:
                    act.wait_ge(consts, 12)
                    for t in range(KT):
                        i = nc.scalar.activation(V1[:, b, t, :, 0:D1],
                                                 ps(key, t * C, t * C + C).rearrange("p (h d) -> p h d", h=H), ACT.Copy)
                    i.then_inc(free_of(key), 1)

            def probs(l, b):
                for u in range(4):
                    key = (f"t{u}", l, b)
                    filled(act, key)
                    c, n = (512 * u, 512) if l == 0 or u < 2 else (512 + T * u, T)
                    nc.scalar.activation(pr[:, b, c:c + n], ps(key, 0, n), ACT.Exp,
                                         scale=SCALE[l]).then_inc(free_of(key), 1)

            def values(l, b):
                key = ("pv", l, b)
                filled(act, key)
                nc.scalar.activation(rden[:, b, :], ps(key, T, 2 * T), ACT.Ln).then_inc(S["lden", l], 1)
                act.wait_ge(S["lden", l], b + 1)
                nc.scalar.activation(rden[:, b, :], rden[:, b, :], ACT.Exp, scale=-1.0).then_inc(S["rden", l], 1)

            run = {"center": center, "scale": scale, "newton": newton, "project": project, "probs": probs,
                   "values": values}
            for step, l, b in ORDER:
                if step in run:
                    run[step](l, b)

            def gelus(k):
                filled(act, ("h", k))
                if k >= 3:
                    e, j = divmod(k - 3, FT)
                    if j == FT - 1:
                        filled(act, ("y", e))
                    else:
                        act.wait_ge(hused, e + 1)
                nc.scalar.activation(hid[:, k % 3, :, :], bank[:, 2 * (k % 2):2 * (k % 2) + 2, :], ACT.Gelu,
                                     bias=b1c[:, k:k + 1]).then_inc(free_of(("h", k)), 1)

            def outputs(e):
                filled(act, ("y", e))
                if e >= 2:
                    read_out(act, ("w", e - 2))
                nc.scalar.activation(ye[:, e % 2, :], ps(("y", e)), ACT.Identity, bias=b2c[:, e:e + 1]).then_inc(free_of(("y", e)), 1)

            for k in range(NK):
                gelus(k)
                if k == 0:
                    act.wait_ge(gsteps, 3)
                    nc.scalar.activation(th[:, :], df[:, :], ACT.Tanh, scale=0.5).then_inc(tanh, 1)
                if k == 2:
                    filled(act, "gate_t")
                    nc.scalar.activation(wT[:, 0, :], ps("gate_t", p1=2 * E), ACT.Copy).then_inc(wt_hi, 1)
                if k % FT == 0 and k >= FT:
                    outputs(k // FT - 1)
            outputs(E - 1)
            act.wait_ge(result, 1)
            act.dma_start(oo[:, 2:4, :], acc[C:P, :].rearrange("p (b t) -> p b t", b=2)).then_inc(stored, 16)
            act.wait_ge(stored, 32)

        @block.vector
        def _(dve):
            nc.vector.memset(onesf[:, :], 1.0)
            nc.vector.memset(onesc[:, :], 1.0)
            nc.vector.memset(avg[:, :], 1.0 / P)
            for l in range(3):
                nc.vector.memset(eps[:, l:l + 1], EPS[l])
            nc.vector.memset(half[:, :], 0.5).then_inc(cst, 1)
            dve.wait_ge(cst, 1)
            nc.vector.tensor_copy(onesr[:, :], onesc[:, :]).then_inc(cst, 1)
            dve.wait_ge(consts, 6)
            nc.vector.tensor_copy(identb[:, :], ident[:, :]).then_inc(cst, 1)
            nc.vector.tensor_reduce(lows[:, 0:1], ident[:, C:P], AX.X, ALU.add, negate=True)
            nc.vector.tensor_reduce(lows[:, 1:2], ident[:, :].rearrange("p (a r c) -> p a r c", r=2, c=16)[:, :, 1, :],
                                    AX.XY, ALU.add, negate=True)
            nc.vector.tensor_reduce(lows[:, 2:3], ident[:, :].rearrange("p (a r c) -> p a r c", r=2, c=32)[:, :, 1, :],
                                    AX.XY, ALU.add, negate=True).then_inc(cst, 1)
            for e in range(E):
                for s in range(2):
                    i = nc.vector.tensor_copy(sel[:, e, s, :], ident[0:2 * E, E * s + e:E * s + e + 1].to_broadcast([2 * E, C]))
            i.then_inc(cst, 1)

            dve.wait_ge(ld["x"], 32)
            for b in range(B):
                i = nc.vector.bn_stats(st6[:, b, :], X[:, b, :])
            i.then_inc(stats, 1)
            dve.wait_ge(stats, 1)
            for b in range(B):
                i = nc.vector.bn_aggr(mv[:, b, :], st6[:, b, :])
            i.then_inc(stats, 1)
            dve.wait_ge(ld["a"], 32)
            for t in range(3):
                for r in range(2):
                    i = nc.vector.tensor_tensor(wg0[:, t, r, :], wq0[:, t, :], grow[:, :], ALU.mult)
            i.then_inc(prep_v, 1)
            filled(dve, "group")
            nc.vector.tensor_copy(gmv[:, :, :], ps("group", 0, 2 * B).rearrange("p (b s) -> p b s", s=2)).then_inc(free_of("group"), 1)
            dve.wait_ge(free_of("group"), 1)
            nc.vector.tensor_tensor(gt[:, 0, :], mv[:, :, 0], gmv[:, :, 0], ALU.subtract).then_inc(stats, 1)
            dve.wait_ge(stats, 3)
            link = sem("group_chain")
            nc.vector.tensor_tensor(gt[:, 1, :], gt[:, 0, :], gt[:, 0, :], ALU.mult).then_inc(link, 1)
            dve.wait_ge(link, 1)
            nc.vector.scalar_tensor_tensor(gt[:, 2, :], gt[:, 1, :], GN_EPS, gmv[:, :, 1], ALU.add, ALU.add).then_inc(stats, 1)
            dve.wait_ge(gact, 2)
            nc.vector.tensor_tensor(gt[:, 4, :], gt[:, 3, :], gt[:, 3, :], ALU.mult).then_inc(link, 1)
            dve.wait_ge(link, 2)
            nc.vector.tensor_tensor(gt[:, 5, :], gt[:, 4, :], gt[:, 2, :], ALU.mult).then_inc(link, 1)
            dve.wait_ge(link, 3)
            nc.vector.tensor_scalar(gt[:, 4, :], gt[:, 5, :], -0.5, 1.5, ALU.mult, ALU.add).then_inc(link, 1)
            dve.wait_ge(link, 4)
            nc.vector.tensor_tensor(gt[:, 0, :], gt[:, 3, :], gt[:, 4, :], ALU.mult).then_inc(link, 1)
            dve.wait_ge(link, 5)
            nc.vector.scalar_tensor_tensor(gt[:, 1, :], gmv[:, :, 0], -1.0, gt[:, 0, :], ALU.mult, ALU.mult).then_inc(link, 1)
            dve.wait_ge(link, 6)

            dve.wait_ge(cst, 4)
            dve.wait_ge(prep_a, 1)
            for h in range(H):
                nc.vector.scalar_tensor_tensor(m_st[:, h, :], f32(m_hi[:, h, :]), lows[:, 0:1],
                                               ps(("prep_m", h), 0, P), ALU.mult, ALU.add).then_inc(free_of(("prep_m", h)), 1)
            dve.wait_ge(prep_a, 5)
            nc.vector.scalar_tensor_tensor(v_st[:, :], f32(v_hi[:, :]), lows[:, 0:1], ps("prep_t", 0, P),
                                           ALU.mult, ALU.add).then_inc(free_of("prep_t"), 1)

            def prep_layer1():
                dve.wait_ge(ld["c"], 7 * 16)
                nc.vector.tensor_copy(w_hi[:, :, :], w_raw[:, :, :]).then_inc(prep_v, 1)
                dve.wait_ge(prep_v, 2)
                nc.vector.scalar_tensor_tensor(w_st[:, :, :], f32(w_hi[:, :, :]), lows[:, 0:1], w_raw[:, :, :],
                                               ALU.mult, ALU.add).then_inc(prep_v, 1)

            def center(l, b):
                if l == 0:
                    nc.vector.tensor_scalar(dev[:, b, :], X[:, b, :], gt[:, 0, b:b + 1], gt[:, 1, b:b + 1],
                                            ALU.mult, ALU.add).then_inc(S["dev", 0], 1)
                else:
                    key = ("mean", l, b)
                    filled(dve, key)
                    nc.vector.tensor_tensor(dev[:, b, :], X[:, b, :], ps(key, 0, T), ALU.subtract).then_inc(free_of(key), 1)

            def newton(l, b):
                key = ("var", l, b)
                dve.wait_ge(S["rs2", l], b + 1)
                nc.vector.scalar_tensor_tensor(rs2[:, b, :], ps(key, 0, T), EPS[l], rs2[:, b, :],
                                               ALU.add, ALU.mult).then_inc(free_of(key), 1)
                read_out(dve, key)
                dve.wait_ge(S["xr", l], b + 1)
                nc.vector.scalar_tensor_tensor(xm[:, b, :], rs2[:, b, :], -3.0, xm[:, b, :], ALU.add, ALU.mult).then_inc(S["xm", l], 1)

            def split(l, b):
                dve.wait_ge(S["X1", l], b + 1)
                nc.vector.scalar_tensor_tensor(X2[:, b, :], xm[:, b, :], -0.5, f32(X1[:, b, :]),
                                               ALU.mult, ALU.subtract).then_inc(S["X2", l], 1)

            def project(l, b):
                for u in range(2):
                    key = (f"y{u}", l, b)
                    dve.wait_ge(S["yhi"], 2 * number[l, b] + u + 1)
                    low = lows[:, 0:1] if l == 0 else lows[:, 1 + u:2 + u]
                    nc.vector.scalar_tensor_tensor(Y[:, b, u, :], f32(yhi[:, u, :]), low, ps(key),
                                                   ALU.mult, ALU.add).then_inc(free_of(key), 1)

            def maxima(l, b):
                for u in range(4):
                    key = (f"s{u}", l, b)
                    filled(dve, key)
                    if l == 0:
                        o, i = mx[:, b, u, :], ps(key).rearrange("p (q t) -> p q t", q=KT)
                    else:
                        q, n = u // 2, P * (u // 2 + 1)
                        o = mx[:, b, :, q].rearrange("p (a r) -> p r a", r=2)[:, u % 2, :]
                        i = ps(key, 0, 2 * n).rearrange("p (h t) -> p h t", h=2)
                    nc.vector.tensor_reduce(o, i, AX.X, ALU.max).then_inc(free_of(key), 1)

            def values(l, b):
                key = ("pv", l, b)
                dve.wait_ge(S["rden", l], b + 1)
                nc.vector.tensor_tensor(dr[:, b, :], ps(key, T, 2 * T), rden[:, b, :], ALU.mult).then_inc(S["dr", l], 1)
                nc.vector.tensor_tensor(att[:, b, :], ps(key, 0, T), rden[:, b, :], ALU.mult).then_inc(free_of(key), 1)
                dve.wait_ge(S["dr", l], b + 1)
                read_out(dve, key)
                nc.vector.scalar_tensor_tensor(att[:, b, :], dr[:, b, :], 2.0, att[:, b, :], ALU.subtract,
                                               ALU.mult).then_inc(S["att", l], 1)

            def residual(l, b):
                key = ("o", l, b)
                filled(dve, key)
                if (l, b) == (0, 0):
                    dve.wait_ge(ld["b"], 16 * (4 + 2 * H))
                nc.vector.scalar_tensor_tensor(X[:, b, :], X[:, b, :], bcol[:, l:l + 1], ps(key, 0, T),
                                               ALU.add, ALU.subtract).then_inc(free_of(key), 1)

            def gate(l, b):
                key = ("logits", l, b)
                filled(dve, key)
                nc.vector.tensor_tensor(lg[:, KT * b:KT * b + KT, :], ps(key, 0, KT * E).rearrange("p (t e) -> p t e", e=E),
                                        bgate[:, :].rearrange("p (o e) -> p o e", o=1).to_broadcast([P, KT, E]),
                                        ALU.add).then_inc(free_of(key), 1)

            run = {"center": center, "newton": newton, "split": split, "project": project, "maxima": maxima,
                   "values": values, "residual": residual, "gate": gate}
            for step, l, b in ORDER:
                if step in run:
                    run[step](l, b)
                if (step, l, b) == ("project", 0, 0):
                    prep_layer1()

            for b in range(B):
                read_out(dve, ("logits", 2, b))
            for t in range(TT):
                i = nc.vector.max(m8[:, t, :], lg[:, t, :])
            i.then_inc(gsteps, 1)
            dve.wait_ge(gsteps, 1)
            for t in range(TT):
                i = nc.vector.max_index(i8[:, t, :], m8[:, t, :], lg[:, t, :])
            i.then_inc(gsteps, 1)
            nc.vector.tensor_tensor(df[:, :], m8[:, :, 0], m8[:, :, 1], ALU.subtract).then_inc(gsteps, 1)
            dve.wait_ge(gsteps, 2)
            for s in range(2):
                i = nc.vector.tensor_copy(i2[:, s, :], i8[:, :, s])
            i.then_inc(gsteps, 1)
            dve.wait_ge(tanh, 1)
            nc.vector.tensor_scalar(wt[:, 0, :], th[:, :], 0.5, 0.5, ALU.mult, ALU.add)
            nc.vector.tensor_scalar(wt[:, 1, :], th[:, :], -0.5, 0.5, ALU.mult, ALU.add).then_inc(gsteps, 1)
            dve.wait_ge(gsteps, 5)
            for s in range(2):
                i = nc.vector.tensor_tensor(eq[:, s, :, :], iota[:, :].rearrange("p (o e) -> p o e", o=1).to_broadcast([P, TT, E]),
                                            i2[:, s, :].rearrange("p (t o) -> p t o", o=1).to_broadcast([P, TT, E]), ALU.is_equal)
            i.then_inc(gsteps, 1)
            dve.wait_ge(gsteps, 6)
            for s in range(2):
                i = nc.vector.tensor_tensor(eq[:, s, :, :], eq[:, s, :, :],
                                            wt[:, s, :].rearrange("p (t o) -> p t o", o=1).to_broadcast([P, TT, E]), ALU.mult)
            i.then_inc(gsteps, 1)
            dve.wait_ge(gsteps, 7)
            ev = eq[:, :, :, :].rearrange("p s (a j) e -> p s a j e", a=2)
            for a in range(2):
                i = nc.vector.tensor_tensor(wd[:, :, a, :], ev[:, 0, a, :, :], ev[:, 1, a, :, :], ALU.add)
            i.then_inc(gsteps, 1)
            dve.wait_ge(wt_hi, 1)
            nc.vector.tensor_tensor(wT[:, 1, :], ps("gate_t", p1=2 * E), f32(wT[:, 0, :]), ALU.subtract).then_inc(free_of("gate_t"), 1)

            for e in range(E):
                read_out(dve, ("y", e))
                filled(dve, ("w", e))
                if e >= 2:
                    dve.wait_ge(summed, e)
                nc.vector.tensor_tensor(yw[:, e % 2, :], ye[:, e % 2, :], ps(("w", e)), ALU.mult).then_inc(free_of(("w", e)), 1)
            dve.wait_ge(summed, E)
            read_out(dve, ("w", E - 1))
            nc.vector.tensor_tensor(acc[:, :], acc[:, :], yw[:, (E - 1) % 2, :], ALU.add).then_inc(result, 1)

        @block.tensor
        def _(pe):
            mm = nc.tensor.matmul
            pe.wait_ge(consts, 10)
            pe.wait_ge(stats, 2)
            mm(ps("group", 0, 2 * B), pair[:, :], mv[:, :, :].rearrange("p b s -> p (b s)"), start=True, stop=True).then_inc(full_of("group"), 1)
            pe.wait_ge(prep_v, 1)
            for h in range(H):
                mm(ps(("prep_m", h), 0, P), wg0[D0 * h:D0 * h + D0, 0, :, :].rearrange("p r c -> p (r c)"),
                       wg0[D0 * h:D0 * h + D0, 1, :, :].rearrange("p r c -> p (r c)"), start=True,
                   stop=True).then_inc(full_of(("prep_m", h)), 1)
            pe.wait_ge(ld["g"], 16 * 5)
            nc.tensor.transpose(ps("prep_t", 0, P), wg0[:, 2, :, :].rearrange("p r c -> p (r c)"), ident[:, :])
            nc.tensor.transpose(ps("prep_t", P, 2 * P), wo0[:, :], ident[:, :])
            nc.tensor.transpose(ps("prep_t", 2 * P, 2 * P + NK), b1_raw[:, :], ident[0:NK, 0:NK])
            nc.tensor.transpose(ps("prep_t", 3 * P, 3 * P + E), b2_raw[:, :, :].rearrange("p r c -> p (r c)"),
                                ident[0:E, 0:E]).then_inc(full_of("prep_t"), 1)

            def center(l, b):
                if l:
                    key = ("mean", l, b)
                    claim(pe, key)
                    read_out(pe, ("o", l - 1, b))
                    mm(ps(key, 0, T), avg[:, :], X[:, b, :], start=True, stop=True).then_inc(full_of(key), 1)

            def scale(l, b):
                key = ("var", l, b)
                claim(pe, key)
                pe.wait_ge(S["sq", l], b + 1)
                mm(ps(key, 0, T), avg[:, :], sq[:, b, :], start=True, stop=True).then_inc(full_of(key), 1)

            def project(l, b):
                pe.wait_ge(S["X1", l], b + 1)
                pe.wait_ge(S["X2", l], b + 1)
                for u in range(2):
                    key = (f"y{u}", l, b)
                    claim(pe, key)
                    if b == 0 and l == 0:
                        for v in range(2):
                            pe.wait_ge(free_of(("prep_m", 2 * u + v)), 1)
                    elif b == 0:
                        pe.wait_ge(prep_g, 4)
                    for v in range(2):
                        o = ps(key, T * v, T * v + T)
                        if l == 0:
                            w = m_st[:, 2 * u + v, :]
                            mm(o, w, X1[:, b, :], start=True, stop=False)
                            i = mm(o, w, X2[:, b, :], start=False, stop=True)
                        else:
                            heads = slice(H * u + 2 * v, H * u + 2 * v + 2)
                            w, bias = (w_qk[:, s, heads, :, :].rearrange("p h r d -> p (h r d)") for s in range(2))
                            mm(o, w, X1[:, b, :], start=True, stop=False)
                            mm(o, w, X2[:, b, :], start=False, stop=False)
                            i = mm(o, bias, onesr[:, :], start=False, stop=True)
                    i.then_inc(full_of(key), 1)
                key = ("v", l, b)
                claim(pe, key)
                if l == 0 and b == 0:
                    pe.wait_ge(free_of("prep_t"), 1)
                for t in range(KT):
                    tok = slice(P * t, P * t + P)
                    if l == 0:
                        o = ps(key, P * t, P * t + P)
                        mm(o, X1[:, b, tok], v_st[:, :], start=True, stop=False)
                        i = mm(o, X2[:, b, tok], v_st[:, :], start=False, stop=True)
                    else:
                        o = ps(key, C * t, C * t + C)
                        mm(o, X1[:, b, tok], w_st[:, 0, 2 * C:3 * C], start=True, stop=False)
                        mm(o, X2[:, b, tok], w_st[:, 0, 2 * C:3 * C], start=False, stop=False)
                        i = mm(o, onesr[:, 0:P], w_st[:, 1, 2 * C:3 * C], start=False, stop=True)
                i.then_inc(full_of(key), 1)

            def q1(b, h, t0, t1):
                p = C * (h % 2)
                return Y[p:p + C, b, 0, T * (h // 2) + t0:T * (h // 2) + t1]

            def k1(b, h, t0, t1):
                p = C * (h % 2)
                return Y[p:p + C, b, 1, T * (h // 2) + t0:T * (h // 2) + t1]

            def maxima(l, b):
                if l == 0:
                    for h in range(H):
                        key = (f"s{h}", l, b)
                        claim(pe, key)
                        if h % 2 == 0:
                            read_out(pe, (f"y{h // 2}", l, b))
                        for q in range(KT):
                            c = T * (h % 2) + P * q
                            i = mm(ps(key, T * q, T * q + T), Y[:, b, h // 2, c:c + P], X1[:, b, :], start=True, stop=True)
                        i.then_inc(full_of(key), 1)
                    return
                read_out(pe, ("y0", l, b))
                read_out(pe, ("y1", l, b))
                for u in range(4):
                    key = (f"s{u}", l, b)
                    claim(pe, key)
                    q, n = u // 2, P * (u // 2 + 1)
                    for v in range(2):
                        h = u % 2 + 2 * v
                        mm(ps(key, n * v, n * v + n), q1(b, h, P * q, P * q + P), k1(b, h, 0, n), start=True, stop=False)
                        i = mm(ps(key, n * v + n - P, n * v + n), identb[:, :], cmask[:, 0, :], start=False, stop=True)
                    i.then_inc(full_of(key), 1)

            def probs(l, b):
                if l == 0:
                    for h in range(H):
                        key = (f"t{h}", l, b)
                        claim(pe, key)
                        pe.wait_ge(S["diag", l], 8 * b + 2 * h + 2)
                        y = Y[:, b, h // 2, T * (h % 2):T * (h % 2) + T]
                        for t in range(KT):
                            tok = slice(P * t, P * t + P)
                            o = ps(key, T * t, T * t + T)
                            mm(o, X1[:, b, tok], y, start=True, stop=False)
                            mm(o, X2[:, b, tok], y, start=False, stop=False)
                            i = mm(o, onesr[:, 0:P], diag[:, b, h, :, :].rearrange("p q c -> p (q c)"), start=False, stop=True)
                        i.then_inc(full_of(key), 1)
                    return
                for u in range(4):
                    key = (f"t{u}", l, b)
                    claim(pe, key)
                    pe.wait_ge(S["diag", l], 8 * b + (6, 8, 8, 8)[u])
                    k0 = P * (u // 2)
                    n = T - k0
                    for v in range(2):
                        h = u % 2 + 2 * v
                        o = ps(key, n * v, n * v + n)
                        mm(o, k1(b, h, k0, k0 + P), q1(b, h, k0, T), start=True, stop=False)
                        mm(ps(key, n * v, n * v + P), identb[:, :], cmask[:, 1, :], start=False, stop=False)
                        i = mm(o, onesr[:, 0:P], diag[:, b, h, u // 2:KT, :].rearrange("p q c -> p (q c)"), start=False, stop=True)
                    i.then_inc(full_of(key), 1)

            def values(l, b):
                for u in range(4):
                    read_out(pe, (f"t{u}", l, b))
                read_out(pe, ("v", l, b))
                key = ("pv", l, b)
                claim(pe, key)
                for den in range(2):
                    for t in range(KT):
                        for h in range(H):
                            if l == 0:
                                w, p, q0 = V0[:, b, t, D0 * h:D0 * h + D0], pr[:, b, 512 * h + T * t:512 * h + T * t + T], 0
                            elif t == 0:
                                c = 512 * (h % 2) + T * (h // 2)
                                w, p, q0 = V1[:, b, t, h, :], pr[:, b, c:c + T], 0
                            else:
                                c = 1024 + T * (h % 2) + P * (h // 2)
                                w, p, q0 = V1[:, b, t, h, :], pr[:, b, c:c + P], P
                            if den:
                                w = onesf[:, :]
                            i = mm(ps(key, T * den + q0, T * den + T, 32 * h, 32 * h + 32), w, p,
                                   start=(t == 0), stop=(t == KT - 1))
                i.then_inc(full_of(key), 1)

            def residual(l, b):
                key = ("o", l, b)
                claim(pe, key)
                if b == 0 and l == 1:
                    pe.wait_ge(ld["b"], 16 * (4 + 2 * H))
                pe.wait_ge(S["att", l], b + 1)
                w = wo0t[:, :] if l == 0 else wo1t[:, :, :].rearrange("p r c -> p (r c)")
                mm(ps(key, 0, T), w, att[:, b, :], start=True, stop=True).then_inc(full_of(key), 1)

            def gate(l, b):
                key = ("logits", l, b)
                claim(pe, key)
                pe.wait_ge(S["X1", l], b + 1)
                for t in range(KT):
                    tok, o = slice(P * t, P * t + P), ps(key, E * t, E * t + E)
                    mm(o, X1[:, b, tok], w_st[:, 0, 3 * C:NW], start=True, stop=False)
                    if t == 0:
                        pe.wait_ge(S["X2", l], b + 1)
                    i = mm(o, X2[:, b, tok], w_st[:, 0, 3 * C:NW], start=False, stop=True)
                i.then_inc(full_of(key), 1)

            run = {"center": center, "scale": scale, "project": project, "maxima": maxima, "probs": probs,
                   "values": values, "residual": residual, "gate": gate}
            for step, l, b in ORDER:
                if step in run:
                    run[step](l, b)

            pe.wait_ge(S["X2", 2], B)
            pe.wait_ge(prep_g, 12)

            def up(k):
                key = ("h", k)
                claim(pe, key)
                if k < 2:
                    pe.wait_ge(free[use[key][0] + 1], ring_used[use[key][0] + 1])
                for s in range(2):
                    w = w1_st[:, P * k:P * k + P]
                    o = bank[:, use[key][0] + s, :]
                    x1, x2 = (G[:, 2 * s:2 * s + 2, :].rearrange("p b t -> p (b t)") for G in (X1, X2))
                    mm(o, w, x1, start=True, stop=False)
                    i = mm(o, w, x2, start=False, stop=True)
                i.then_inc(full_of(key), 1)

            def down(k):
                e, j = divmod(k, FT)
                key = ("y", e)
                if j == 0:
                    claim(pe, key)
                read_out(pe, ("h", k))
                for s in range(2):
                    i = mm(ps(key, p0=C * s, p1=C * s + C), w2_sb[:, k, :], hid[:, k % 3, s, :],
                           start=(j == 0), stop=(j == FT - 1))
                i.then_inc(*((full_of(key), 1) if j == FT - 1 else (hused, 1)))

            def spread(e):
                key = ("w", e)
                claim(pe, key)
                if e == 0:
                    pe.wait_ge(free_of("gate_t"), use["gate_t"][1] + 1)
                w = sel[:, e, :, :].rearrange("p s c -> p (s c)")
                mm(ps(key), w, wT[:, 0, :], start=True, stop=False)
                mm(ps(key), w, wT[:, 1, :], start=False, stop=True).then_inc(full_of(key), 1)

            up(0)
            pe.wait_ge(ld["w2"], 16)
            for k in range(NK):
                if k + 1 < NK:
                    up(k + 1)
                if k == 1:
                    claim(pe, "gate_t")
                    pe.wait_ge(gsteps, 8)
                    for j in range(TT // 2):
                        i = nc.tensor.transpose(ps("gate_t", P * j, P * j + P, p1=2 * E),
                                                wd[:, j, :, :].rearrange("p s e -> p (s e)"), ident[:, :])
                    i.then_inc(full_of("gate_t"), 1)
                down(k)
                if k >= 3 and k % 2 == 1:
                    spread((k - 3) // 2)
            spread(E - 1)


_INS = ['x', 'L0_conv_g', 'L0_conv_w_qkv', 'L0_conv_w_out', 'L0_conv_b_out', 'L1_attn_W_qkv', 'L1_attn_b_qkv',
        'L1_attn_W_out', 'L1_attn_b_out', 'L1_ffn_Wg', 'L1_ffn_bg', 'L1_ffn_W1', 'L1_ffn_b1', 'L1_ffn_W2', 'L1_ffn_b2']
_OUTS = [((4, 64, 16, 16), 'float32')]


def kernel(**inputs):
    import numpy as _np
    import concourse.bacc as _bacc
    from concourse import mybir as _mybir
    from concourse.bass_utils import run_bass_kernel_spmd as _run

    nc = _bacc.Bacc("TRN2", target_bir_lowering=False, num_devices=1)
    arrays, args = {}, []
    for name in _INS:
        a = _np.ascontiguousarray(inputs[name])
        arrays[f"in_{name}_dram"] = a
        args.append(nc.dram_tensor(f"in_{name}_dram", a.shape, _mybir.dt.from_np(a.dtype), kind="ExternalInput").ap())
    for i, (shape, dtype) in enumerate(_OUTS):
        dt = _mybir.dt.from_np(_np.dtype(dtype))
        args.append(nc.dram_tensor(f"out_{i}_dram", shape, dt, kind="ExternalOutput").ap())
    hybrid_block(nc, *args)
    r = _run(nc, [arrays], core_ids=[0])
    return r.results[0]["out_0_dram"]
```

```python
from contextlib import ExitStack

import concourse.bass as bass
from concourse import mybir

F32 = mybir.dt.float32
F32R = mybir.dt.float32r
BF16 = mybir.dt.bfloat16
U32 = mybir.dt.uint32
ALU = mybir.AluOpType
ACT = mybir.ActivationFunctionType
AX = mybir.AxisListType

P = 128
MASKED = -1e30
CHAIN = [(step, layer) for layer in (0, 1) for step in
         ("center", "scale", "newton", "split", "project", "maxima", "probs", "values", "residual")]
CHAIN += [(step, 2) for step in ("center", "scale", "newton", "split", "gate")]
STARTS = ((0, 0, 0, 2),
          (2, 4, 8, 8),
          (6, 10, 12, 16),
          (14, 18, 18, 22),
          (20, 20, 26, 26),
          (24, 28, 30, 34),
          (28, 34, 38, 38),
          (32, 40, 42, 42),
          (36, 44, 46, 48),
          (46, 50, 50, 50),
          (46, 50, 52, 54),
          (54, 56, 56, 60),
          (58, 62, 62, 62),
          (64, 66, 70, 70),
          (68, 72, 76, 76),
          (74, 80, 80, 88),
          (78, 84, 86, 94),
          (82, 92, 100, 102),
          (90, 96, 104, 104),
          (98, 98, 106, 108),
          (102, 106, 110, 110),
          (108, 108, 112, 112),
          (112, 114, 116, 118))


def schedule(starts):
    order = sorted((starts[i][b], b, i) for i in range(len(CHAIN)) for b in range(len(starts[i])))
    return [(*CHAIN[i], b) for _, b, i in order]


def hybrid_block(nc, x, g0, wqkv0, wout0, bout0, wqkv1, bqkv1, wout1, bout1, wg, bg, w1, b1, w2, b2, out):
    B, C, HH, WW = x.shape
    T = HH * WW
    H = 4
    D0 = wqkv0.shape[0] // 3 // H
    D1 = wqkv1.shape[1] // 3 // H
    E, _, F = w1.shape
    KT = T // P
    FT = F // P
    NK = E * FT
    TT = B * T // P
    HALF = B * T // 2
    assert (B, C, T, H, D0, D1, E, F) == (4, 64, 256, 4, 32, 16, 8, 256)
    SCALE = (float(D0) ** -0.5, float(D1) ** -0.5)
    EPS = (1e-12, 1e-5, 1e-5)
    GN_EPS = 1e-5
    ORDER = schedule(STARTS)
    SPREAD_AT = [max(e + 3, FT * e) for e in range(E)]

    use, used = {}, [0] * 8

    def take(key, bank):
        use[key] = (bank, used[bank])
        used[bank] += 1

    for h in range(H):
        take(("prep_m", h), 4 + h)
    take("prep_t", 3)
    take("group", 2)
    turn = 0
    for step, layer, b in ORDER:
        names = {
            "center": ["norm"],
            "scale": [],
            "newton": [],
            "split": [],
            "project": ["y0", "y1", "v"],
            "maxima": ["s0", "s1", "s2", "s3"],
            "probs": ["t0", "t1", "t2", "t3"],
            "values": ["pv"],
            "residual": ["o"],
            "gate": ["logits"],
        }[step]
        for name in names:
            take((name, layer, b), turn % 8)
            turn += 1
    ring_used = list(used)
    for k in range(NK):
        take(("h", k), 2 * (k % 2))
    take("gate_t", 7)
    for e in range(E):
        take(("y", e), 4 + e % 2)
        take(("w", e), 6 + e % 2)

    projections = [(l, b) for step, l, b in ORDER if step == "project"]
    number = {key: n for n, key in enumerate(projections)}
    before = dict(zip(projections[1:], projections))

    with ExitStack() as ctx:
        def sb(name, shape, dt=F32):
            return ctx.enter_context(nc.sbuf_tensor(name, shape, dt))

        sems = {}

        def sem(name):
            if name not in sems:
                sems[name] = ctx.enter_context(nc.semaphore(name))
            return sems[name]

        bank = ctx.enter_context(nc.psum_tensor("bank", [P, 8, 512], F32))
        full = [sem(f"psum_full{i}") for i in range(8)]
        free = [sem(f"psum_free{i}") for i in range(8)]

        def ps(key, lo=0, hi=512, p0=0, p1=P):
            return bank[p0:p1, use[key][0], lo:hi]

        def claim(pe, key):
            k, n = use[key]
            if n:
                pe.wait_ge(free[k], n)

        def filled(eng, key):
            k, n = use[key]
            eng.wait_ge(full[k], n + 1)

        def read_out(eng, key):
            k, n = use[key]
            eng.wait_ge(free[k], n + 1)

        def full_of(key):
            return full[use[key][0]]

        def free_of(key):
            return free[use[key][0]]

        X = sb("x", [P, B, T])
        dev = sb("dev", [P, B, T])
        sq = sb("sq", [P, B, T])
        rs2 = sb("rs2", [P, B, T])
        xm = sb("xm", [P, B, T])
        X1 = sb("X1", [P, B, T], F32R)
        X2 = sb("X2", [P, B, T], F32R)
        yhi = sb("yhi", [P, 2, 512], F32R)
        Y = sb("Y", [P, B, 2, 512], F32R)
        V0 = sb("V0", [P, B, KT, P])
        V1 = sb("V1", [P, B, KT, H, 32])
        mx = sb("mx", [P, B, H, KT])
        diag = sb("diag", [P, B, H, KT, P], F32R)
        pr = sb("pr", [P, B, H * KT * T])
        rden = sb("rden", [P, B, T])
        dr = sb("dr", [P, B, T])
        att = sb("att", [P, B, T])
        ident = sb("ident", [P, P])
        identb = sb("identb", [P, P], BF16)
        cmask = sb("cmask", [P, 2, P], BF16)
        onesf = sb("onesf", [P, 32])
        onesc = sb("onesc", [P, T])
        onesr = sb("onesr", [P, T], F32R)
        avg = sb("avg", [P, P])
        centering = sb("centering", [P, P])
        pair = sb("pair", [P, P])
        lows = sb("lows", [P, 3])
        eps = sb("eps", [P, 3])
        iota = sb("iota", [P, E])
        sel = sb("sel", [2 * E, E, 2, C], F32R)
        st6 = sb("st6", [P, B, 6])
        mv = sb("mv", [P, B, 2])
        gt = sb("gt", [P, 6, B])
        grow = sb("grow", [P, C])
        wq0 = sb("wq0", [P, 3, C])
        wg0 = sb("wg0", [P, 3, 2, C])
        m_hi = sb("m_hi", [P, H, P], F32R)
        m_st = sb("m_st", [P, H, P], F32R)
        v_hi = sb("v_hi", [P, P], F32R)
        v_st = sb("v_st", [P, P], F32R)
        wo0 = sb("wo0", [P, P])
        wo0t = sb("wo0t", [P, P])
        bcol = sb("bcol", [P, 2])
        NW = 3 * C + E
        w_raw = sb("w_raw", [P, 2, NW])
        w_hi = sb("w_hi", [P, 2, NW], F32R)
        w_st = sb("w_st", [P, 2, NW], F32R)
        w_qk = sb("w_qk", [P, 2, 2 * H, 4, D1], F32R)
        wo1t = sb("wo1t", [P, 2, C])
        w1_raw = sb("w1_raw", [P, E, F])
        w1_hi = sb("w1_hi", [P, E * F // 4], F32R)
        w1_st = sb("w1_st", [P, E * F], F32R)
        w2_sb = sb("w2_sb", [P, NK, C])
        b1_raw = sb("b1_raw", [NK, P])
        b2_raw = sb("b2_raw", [E, 2, C])
        b1c = sb("b1c", [P, NK])
        b2c = sb("b2c", [P, E])
        bgate = sb("bgate", [P, E])
        lg = sb("lg", [P, TT, E])
        m8 = sb("m8", [P, TT, 8])
        i8 = sb("i8", [P, TT, 8], U32)
        i2 = sb("i2", [P, 2, TT])
        df = sb("df", [P, TT])
        th = sb("th", [P, TT])
        wt = sb("wt", [P, 2, TT])
        eq = sb("eq", [P, 2, TT, E])
        wd = sb("wd", [P, TT // 2, 2, E])
        wT = sb("wT", [2 * E, 2, HALF], F32R)
        hid = sb("hid", [P, 3, 2, HALF])
        wc = sb("wc", [P, 2, HALF])
        yw = sb("yw", [P, 2, HALF])
        acc = sb("acc", [P, HALF])

        ld = {n: sem("ld_" + n) for n in ("x", "a", "g", "b", "c", "w1", "w2")}
        stored = sem("stored")
        consts = sem("consts")
        cst = sem("cst")
        stats = sem("stats")
        gact = sem("gact")
        prep_v = sem("prep_v")
        prep_g = sem("prep_g")
        prep_a = sem("prep_a")
        S = {(n, l): sem(f"{n}{l}") for l in range(3) for n in
             ("dev", "sq", "lnv", "r0", "rs2", "xr", "xm", "X1", "X2")}
        S |= {(n, l): sem(f"{n}{l}") for l in range(2) for n in
              ("diag", "lden", "rden", "dr", "att")}
        yhi_ready = sem("yhi")
        gsteps = sem("gsteps")
        tanh = sem("tanh")
        wt_hi = sem("wt_hi")
        hused = sem("hused")
        summed = sem("summed")
        result = sem("result")

        block = ctx.enter_context(nc.Block())

        def f32(ap):
            return ap.bitcast(F32)

        xo = x.rearrange("b c h w -> c b (h w)")
        oo = out.rearrange("b c h w -> c b (h w)")

        @block.sync
        def _(sp):
            sp.dma_start(X[0:C, :, :], xo).then_inc(ld["x"], 16)
            sp.dma_start(wo0[0:C, :], wout0).then_inc(ld["g"], 16)
            sp.dma_start(wo0[C:P, :], wout0).then_inc(ld["g"], 16)
            sp.dma_start(b1_raw[:, :], b1.rearrange("e (j p) -> (e j) p", p=P)).then_inc(ld["g"], 16)
            for r in range(2):
                sp.dma_start(b2_raw[:, r, :], b2).then_inc(ld["g"], 16)
            sp.wait_ge(consts, 2)
            for p0 in (0, C):
                sp.dma_start(w_raw[p0:p0 + C, 0, 0:3 * C], wqkv1).then_inc(ld["c"], 16)
                sp.dma_start(w_raw[p0:p0 + C, 0, 3 * C:NW], wg).then_inc(ld["c"], 16)
                sp.dma_start(w_raw[p0:p0 + 1, 1, 0:3 * C], bqkv1.rearrange("(o c) -> o c", o=1)).then_inc(ld["c"], 16)
            sp.dma_start(bgate[:, :], bg.partition_broadcast(P)).then_inc(ld["c"], 16)
            for l, b_ in ((0, bout0), (1, bout1)):
                for p0 in (0, C):
                    sp.dma_start(bcol[p0:p0 + C, l:l + 1], b_.rearrange("(c o) -> c o", o=1)).then_inc(ld["b"], 16)
            for h in range(H):
                for r in range(2):
                    sp.dma_start(wo1t[32 * h:32 * h + D1, r, :], wout1[D1 * h:D1 * h + D1, :]).then_inc(ld["b"], 16)
            for p0 in (0, C):
                sp.dma_start(w1_raw[p0:p0 + C, :, :], w1.rearrange("e c f -> c e f")).then_inc(ld["w1"], 16)
            sp.dma_start(w2_sb[:, :, :], w2.rearrange("e (j p) c -> p (e j) c", p=P)).then_inc(ld["w2"], 16)
            sp.wait_ge(result, 1)
            sp.dma_start(oo[:, 0:2, :], acc[0:C, :].rearrange("p (b t) -> p b t", b=2)).then_inc(stored, 16)
            sp.wait_ge(stored, 32)

        @block.gpsimd
        def _(pool):
            nc.gpsimd.memset(w_raw[:, :, :], 0.0).then_inc(consts, 1)
            nc.gpsimd.memset(wo1t[:, :, :], 0.0).then_inc(consts, 1)
            nc.gpsimd.memset(ident[:, :], 0.0).then_inc(consts, 1)
            nc.gpsimd.memset(pair[:, :], 0.5).then_inc(consts, 1)
            nc.gpsimd.memset(cmask[:, :, :], 0.0).then_inc(consts, 1)
            pool.wait_ge(consts, 5)
            nc.gpsimd.affine_select(out=ident[:, :], in_=ident[:, :], compare_op=ALU.not_equal, fill=1.0,
                                    base=0, pattern=[[-1, P]], channel_multiplier=1).then_inc(consts, 1)
            pv = pair[:, :].rearrange("p (g r) -> p g r", r=2)
            nc.gpsimd.affine_select(out=pv, in_=pv, compare_op=ALU.is_ge, fill=0.0, base=0,
                                    pattern=[[-2, C], [0, 2]], channel_multiplier=1).then_inc(consts, 1)
            nc.gpsimd.affine_select(out=cmask[:, 0, :], in_=cmask[:, 0, :], compare_op=ALU.is_ge, fill=MASKED,
                                    base=0, pattern=[[-1, P]], channel_multiplier=1).then_inc(consts, 1)
            nc.gpsimd.affine_select(out=cmask[:, 1, :], in_=cmask[:, 1, :], compare_op=ALU.is_ge, fill=MASKED,
                                    base=0, pattern=[[1, P]], channel_multiplier=-1).then_inc(consts, 1)
            pool.wait_ge(consts, 7)
            nc.gpsimd.affine_select(out=pv, in_=pv, compare_op=ALU.is_ge, fill=0.0, base=1,
                                    pattern=[[2, C], [0, 2]], channel_multiplier=-1).then_inc(consts, 1)
            nc.gpsimd.iota(iota[:, :], pattern=[[1, E]], base=0, channel_multiplier=0,
                           allow_small_or_imprecise_dtypes=True).then_inc(consts, 1)
            nc.gpsimd.memset(V1[:, :, :, :, :], 0.0).then_inc(consts, 1)

            def repeat_qk():
                pool.wait_ge(prep_v, 3)
                src = w_st[:, :, 0:2 * C].rearrange("p s (h d) -> p s h d", d=D1)
                for r in range(4):
                    nc.gpsimd.tensor_copy(w_qk[:, :, :, r, :], f32(src)).then_inc(prep_g, 1)

            raw = w1_raw[:, :, :].rearrange("p e f -> p (e f)")

            def split_w1(i):
                pool.wait_ge(ld["w1"], 32)
                q = E * F // 4
                c = slice(i * q, (i + 1) * q)
                if i == 0:
                    pool.wait_ge(cst, 4)
                else:
                    pool.wait_ge(prep_g, 4 + 2 * i)
                nc.gpsimd.tensor_scalar(w1_hi[:, :], raw[:, c], lows[:, 0:1], None, ALU.mult).then_inc(prep_g, 1)
                pool.wait_ge(prep_g, 4 + 2 * i + 1)
                nc.gpsimd.tensor_tensor(w1_st[:, c], raw[:, c], f32(w1_hi[:, :]), ALU.add).then_inc(prep_g, 1)

            def scale(l, b):
                pool.wait_ge(S["r0", l], b + 1)
                nc.gpsimd.tensor_tensor(xm[:, b, :], dev[:, b, :], sq[:, b, :], ALU.mult).then_inc(S["xr", l], 1)

            def maxima(l, b):
                for u in range(4):
                    read_out(pool, (f"s{u}", l, b))
                    if l == 0:
                        which = [(u, 0), (u, 1)]
                    else:
                        which = [(u % 2, u // 2), (u % 2 + 2, u // 2)]
                    for h, q in which:
                        nc.gpsimd.tensor_scalar(diag[:, b, h, q, :], ident[:, :], mx[:, b, h, q:q + 1], -1.0,
                                                ALU.mult, ALU.mult).then_inc(S["diag", l], 1)

            n = 0
            for step, l, b in ORDER:
                if step == "scale" and l == 0:
                    scale(l, b)
                if step == "maxima":
                    maxima(l, b)
                    if (l, b) == (0, 0):
                        repeat_qk()
                if step == "residual" and n < 4:
                    split_w1(n)
                    n += 1

            for e in range(E):
                read_out(pool, ("y", e))
                if e == 0:
                    x2 = X[:, :, :]
                    nc.gpsimd.tensor_tensor(acc[0:C, :], yw[0:C, 0, :], x2[0:C, 0:2, :].rearrange("p b t -> p (b t)"), ALU.add).then_inc(summed, 1)
                    pool.wait_ge(summed, 1)
                    nc.gpsimd.tensor_tensor(acc[C:P, :], yw[C:P, 0, :], x2[C:P, 2:4, :].rearrange("p b t -> p (b t)"), ALU.add).then_inc(summed, 1)
                elif e < E - 1:
                    pool.wait_ge(summed, e + 1)
                    nc.gpsimd.tensor_tensor(acc[:, :], acc[:, :], yw[:, e % 2, :], ALU.add).then_inc(summed, 1)

        @block.scalar
        def _(act):
            act.dma_start(X[C:P, :, :], xo).then_inc(ld["x"], 16)
            act.dma_start(wq0[:, :, :], wqkv0.rearrange("(t p) c -> p t c", p=P)).then_inc(ld["a"], 16)
            act.dma_start(grow[:, :], g0.partition_broadcast(P)).then_inc(ld["a"], 16)
            nc.scalar.preload_act_table_set("natural_log_exp_and_others")
            act.wait_ge(stats, 4)
            nc.scalar.activation(gt[:, 3, :], gt[:, 2, :], ACT.Ln).then_inc(gact, 1)
            act.wait_ge(gact, 1)
            nc.scalar.activation(gt[:, 3, :], gt[:, 3, :], ACT.Exp, scale=-0.5).then_inc(gact, 1)
            for h in range(H):
                filled(act, ("prep_m", h))
            nc.scalar.activation(m_hi[:, :, :], bank[:, 4:4 + H, 0:P], ACT.Copy).then_inc(prep_a, 1)

            def prep_transposed():
                filled(act, "prep_t")
                nc.scalar.activation(v_hi[:, :], ps("prep_t", 0, P), ACT.Copy).then_inc(prep_a, 1)
                nc.scalar.activation(wo0t[:, :], ps("prep_t", P, 2 * P), ACT.Copy).then_inc(prep_a, 1)
                nc.scalar.activation(b1c[:, :], ps("prep_t", 2 * P, 2 * P + NK), ACT.Copy).then_inc(prep_a, 1)
                nc.scalar.activation(b2c[:, :], ps("prep_t", 3 * P, 3 * P + E), ACT.Copy).then_inc(prep_a, 1)

            def center(l, b):
                act.wait_ge(S["dev", l], b + 1)
                centred = ps(("norm", l, b), 0, T) if l else dev[:, b, :]
                nc.scalar.activation(sq[:, b, :], centred, ACT.Square).then_inc(S["sq", l], 1)

            def scale(l, b):
                key = ("norm", l, b)
                filled(act, key)
                nc.scalar.activation(sq[:, b, :], ps(key, T, 2 * T), ACT.Ln, bias=eps[:, l:l + 1]).then_inc(S["lnv", l], 1)
                act.wait_ge(S["lnv", l], b + 1)
                nc.scalar.activation(sq[:, b, :], sq[:, b, :], ACT.Exp, scale=-0.5).then_inc(S["r0", l], 1)
                act.wait_ge(S["r0", l], b + 1)
                nc.scalar.activation(rs2[:, b, :], sq[:, b, :], ACT.Square).then_inc(S["rs2", l], 1)

            def newton(l, b):
                act.wait_ge(S["xm", l], b + 1)
                nc.scalar.activation(X1[:, b, :], xm[:, b, :], ACT.Copy, scale=-0.5).then_inc(S["X1", l], 1)

            def project(l, b):
                for u in range(2):
                    key = (f"y{u}", l, b)
                    filled(act, key)
                    if (l, b) in before:
                        read_out(act, (f"y{u}", *before[l, b]))
                    nc.scalar.activation(yhi[:, u, :], ps(key), ACT.Copy).then_inc(yhi_ready, 1)
                key = ("v", l, b)
                filled(act, key)
                if l == 0:
                    nc.scalar.activation(V0[:, b, :, :], ps(key, 0, KT * P).rearrange("p (k c) -> p k c", k=KT),
                                         ACT.Copy).then_inc(free_of(key), 1)
                else:
                    act.wait_ge(consts, 12)
                    for t in range(KT):
                        i = nc.scalar.activation(V1[:, b, t, :, 0:D1],
                                                 ps(key, t * C, t * C + C).rearrange("p (h d) -> p h d", h=H), ACT.Copy)
                    i.then_inc(free_of(key), 1)

            def probs(l, b):
                for u in range(4):
                    key = (f"t{u}", l, b)
                    filled(act, key)
                    c, n = (512 * u, 512) if l == 0 or u < 2 else (512 + T * u, T)
                    nc.scalar.activation(pr[:, b, c:c + n], ps(key, 0, n), ACT.Exp,
                                         scale=SCALE[l]).then_inc(free_of(key), 1)

            def values(l, b):
                key = ("pv", l, b)
                filled(act, key)
                nc.scalar.activation(rden[:, b, :], ps(key, T, 2 * T), ACT.Ln).then_inc(S["lden", l], 1)
                act.wait_ge(S["lden", l], b + 1)
                nc.scalar.activation(rden[:, b, :], rden[:, b, :], ACT.Exp, scale=-1.0).then_inc(S["rden", l], 1)

            run = {"center": center, "scale": scale, "newton": newton, "project": project, "probs": probs,
                   "values": values}
            for step, l, b in ORDER:
                if step in run:
                    run[step](l, b)
                if (step, l, b) == ("center", 0, 1):
                    prep_transposed()

            def gelus(k):
                filled(act, ("h", k))
                if k >= 3:
                    e, j = divmod(k - 3, FT)
                    if j == FT - 1:
                        filled(act, ("y", e))
                    else:
                        act.wait_ge(hused, e + 1)
                nc.scalar.activation(hid[:, k % 3, :, :], bank[:, 2 * (k % 2):2 * (k % 2) + 2, :], ACT.Gelu,
                                     bias=b1c[:, k:k + 1]).then_inc(free_of(("h", k)), 1)

            def spread_out(k):
                for e in range(E):
                    if SPREAD_AT[e] == k:
                        key = ("w", e)
                        filled(act, key)
                        if e >= 2:
                            read_out(act, ("y", e - 2))
                        nc.scalar.activation(wc[:, e % 2, :], ps(key), ACT.Copy).then_inc(free_of(key), 1)

            for k in range(NK):
                gelus(k)
                if k == 0:
                    act.wait_ge(gsteps, 3)
                    nc.scalar.activation(th[:, :], df[:, :], ACT.Tanh, scale=0.5).then_inc(tanh, 1)
                spread_out(k)
                if k == 2:
                    filled(act, "gate_t")
                    nc.scalar.activation(wT[:, 0, :], ps("gate_t", p1=2 * E), ACT.Copy).then_inc(wt_hi, 1)
            act.wait_ge(result, 1)
            act.dma_start(oo[:, 2:4, :], acc[C:P, :].rearrange("p (b t) -> p b t", b=2)).then_inc(stored, 16)
            act.wait_ge(stored, 32)

        @block.vector
        def _(dve):
            nc.vector.memset(onesf[:, :], 1.0)
            nc.vector.memset(onesc[:, :], 1.0)
            nc.vector.memset(avg[:, :], 1.0 / P)
            for l in range(3):
                i = nc.vector.memset(eps[:, l:l + 1], EPS[l])
            i.then_inc(cst, 1)
            dve.wait_ge(cst, 1)
            nc.vector.tensor_copy(onesr[:, :], onesc[:, :]).then_inc(cst, 1)
            dve.wait_ge(consts, 6)
            nc.vector.tensor_copy(identb[:, :], ident[:, :]).then_inc(cst, 1)
            nc.vector.tensor_reduce(lows[:, 0:1], ident[:, C:P], AX.X, ALU.add, negate=True)
            nc.vector.tensor_reduce(lows[:, 1:2], ident[:, :].rearrange("p (a r c) -> p a r c", r=2, c=16)[:, :, 1, :],
                                    AX.XY, ALU.add, negate=True)
            nc.vector.tensor_reduce(lows[:, 2:3], ident[:, :].rearrange("p (a r c) -> p a r c", r=2, c=32)[:, :, 1, :],
                                    AX.XY, ALU.add, negate=True).then_inc(cst, 1)

            dve.wait_ge(ld["x"], 32)
            for b in range(B):
                i = nc.vector.bn_stats(st6[:, b, :], X[:, b, :])
            i.then_inc(stats, 1)
            dve.wait_ge(stats, 1)
            for b in range(B):
                i = nc.vector.bn_aggr(mv[:, b, :], st6[:, b, :])
            i.then_inc(stats, 1)
            dve.wait_ge(ld["a"], 32)
            for t in range(3):
                for r in range(2):
                    i = nc.vector.tensor_tensor(wg0[:, t, r, :], wq0[:, t, :], grow[:, :], ALU.mult)
            i.then_inc(prep_v, 1)
            filled(dve, "group")
            gmv = ps("group", 0, 2 * B).rearrange("p (b s) -> p b s", s=2)
            nc.vector.tensor_tensor(gt[:, 0, :], mv[:, :, 0], gmv[:, :, 0], ALU.subtract).then_inc(stats, 1)
            dve.wait_ge(stats, 3)
            link = sem("group_chain")
            nc.vector.tensor_tensor(gt[:, 1, :], gt[:, 0, :], gt[:, 0, :], ALU.mult).then_inc(link, 1)
            dve.wait_ge(link, 1)
            nc.vector.scalar_tensor_tensor(gt[:, 2, :], gt[:, 1, :], GN_EPS, gmv[:, :, 1], ALU.add, ALU.add).then_inc(stats, 1)
            dve.wait_ge(gact, 2)
            nc.vector.tensor_tensor(gt[:, 4, :], gt[:, 3, :], gt[:, 3, :], ALU.mult).then_inc(link, 1)
            dve.wait_ge(link, 2)
            nc.vector.tensor_tensor(gt[:, 5, :], gt[:, 4, :], gt[:, 2, :], ALU.mult).then_inc(link, 1)
            dve.wait_ge(link, 3)
            nc.vector.tensor_scalar(gt[:, 4, :], gt[:, 5, :], -0.5, 1.5, ALU.mult, ALU.add).then_inc(link, 1)
            dve.wait_ge(link, 4)
            nc.vector.tensor_tensor(gt[:, 0, :], gt[:, 3, :], gt[:, 4, :], ALU.mult).then_inc(link, 1)
            dve.wait_ge(link, 5)
            nc.vector.scalar_tensor_tensor(gt[:, 1, :], gmv[:, :, 0], -1.0, gt[:, 0, :], ALU.mult, ALU.mult).then_inc(free_of("group"), 1)
            read_out(dve, "group")

            for b in range(B):
                nc.vector.tensor_scalar(dev[:, b, :], X[:, b, :], gt[:, 0, b:b + 1], gt[:, 1, b:b + 1],
                                        ALU.mult, ALU.add).then_inc(S["dev", 0], 1)

            dve.wait_ge(cst, 4)
            dve.wait_ge(prep_a, 1)
            for h in range(H):
                nc.vector.scalar_tensor_tensor(m_st[:, h, :], f32(m_hi[:, h, :]), lows[:, 0:1],
                                               ps(("prep_m", h), 0, P), ALU.mult, ALU.add).then_inc(free_of(("prep_m", h)), 1)
            dve.wait_ge(prep_a, 5)
            nc.vector.scalar_tensor_tensor(v_st[:, :], f32(v_hi[:, :]), lows[:, 0:1], ps("prep_t", 0, P),
                                           ALU.mult, ALU.add).then_inc(free_of("prep_t"), 1)

            def prep_layer1():
                nc.vector.tensor_tensor(centering[:, :], ident[:, :], avg[:, :], ALU.subtract).then_inc(cst, 1)
                for e in range(E):
                    for s in range(2):
                        i = nc.vector.tensor_copy(sel[:, e, s, :], ident[0:2 * E, E * s + e:E * s + e + 1].to_broadcast([2 * E, C]))
                i.then_inc(cst, 1)
                dve.wait_ge(ld["c"], 7 * 16)
                nc.vector.tensor_copy(w_hi[:, :, :], w_raw[:, :, :]).then_inc(prep_v, 1)
                dve.wait_ge(prep_v, 2)
                nc.vector.scalar_tensor_tensor(w_st[:, :, :], f32(w_hi[:, :, :]), lows[:, 0:1], w_raw[:, :, :],
                                               ALU.mult, ALU.add).then_inc(prep_v, 1)

            def newton(l, b):
                key = ("norm", l, b)
                if l:
                    dve.wait_ge(S["r0", l], b + 1)
                    nc.vector.tensor_tensor(xm[:, b, :], ps(key, 0, T), sq[:, b, :], ALU.mult).then_inc(S["xr", l], 1)
                dve.wait_ge(S["rs2", l], b + 1)
                nc.vector.scalar_tensor_tensor(rs2[:, b, :], ps(key, T, 2 * T), EPS[l], rs2[:, b, :],
                                               ALU.add, ALU.mult).then_inc(free_of(key), 1)
                read_out(dve, key)
                dve.wait_ge(S["xr", l], b + 1)
                nc.vector.scalar_tensor_tensor(xm[:, b, :], rs2[:, b, :], -3.0, xm[:, b, :], ALU.add, ALU.mult).then_inc(S["xm", l], 1)

            def split(l, b):
                dve.wait_ge(S["X1", l], b + 1)
                nc.vector.scalar_tensor_tensor(X2[:, b, :], xm[:, b, :], -0.5, f32(X1[:, b, :]),
                                               ALU.mult, ALU.subtract).then_inc(S["X2", l], 1)

            def project(l, b):
                for u in range(2):
                    key = (f"y{u}", l, b)
                    dve.wait_ge(yhi_ready, 2 * number[l, b] + u + 1)
                    low = lows[:, 0:1] if l == 0 else lows[:, 1 + u:2 + u]
                    nc.vector.scalar_tensor_tensor(Y[:, b, u, :], f32(yhi[:, u, :]), low, ps(key),
                                                   ALU.mult, ALU.add).then_inc(free_of(key), 1)

            def maxima(l, b):
                for u in range(4):
                    key = (f"s{u}", l, b)
                    filled(dve, key)
                    if l == 0:
                        o, i = mx[:, b, u, :], ps(key).rearrange("p (q t) -> p q t", q=KT)
                    else:
                        q, n = u // 2, P * (u // 2 + 1)
                        o = mx[:, b, :, q].rearrange("p (a r) -> p r a", r=2)[:, u % 2, :]
                        i = ps(key, 0, 2 * n).rearrange("p (h t) -> p h t", h=2)
                    nc.vector.tensor_reduce(o, i, AX.X, ALU.max).then_inc(free_of(key), 1)

            def values(l, b):
                key = ("pv", l, b)
                dve.wait_ge(S["rden", l], b + 1)
                nc.vector.tensor_tensor(dr[:, b, :], ps(key, T, 2 * T), rden[:, b, :], ALU.mult).then_inc(S["dr", l], 1)
                nc.vector.tensor_tensor(att[:, b, :], ps(key, 0, T), rden[:, b, :], ALU.mult).then_inc(free_of(key), 1)
                dve.wait_ge(S["dr", l], b + 1)
                read_out(dve, key)
                nc.vector.scalar_tensor_tensor(att[:, b, :], dr[:, b, :], 2.0, att[:, b, :], ALU.subtract,
                                               ALU.mult).then_inc(S["att", l], 1)

            def residual(l, b):
                key = ("o", l, b)
                filled(dve, key)
                if (l, b) == (0, 0):
                    dve.wait_ge(ld["b"], 16 * (4 + 2 * H))
                nc.vector.scalar_tensor_tensor(X[:, b, :], X[:, b, :], bcol[:, l:l + 1], ps(key, 0, T),
                                               ALU.add, ALU.subtract).then_inc(free_of(key), 1)

            def gate(l, b):
                key = ("logits", l, b)
                filled(dve, key)
                nc.vector.tensor_tensor(lg[:, KT * b:KT * b + KT, :], ps(key, 0, KT * E).rearrange("p (t e) -> p t e", e=E),
                                        bgate[:, :].rearrange("p (o e) -> p o e", o=1).to_broadcast([P, KT, E]),
                                        ALU.add).then_inc(free_of(key), 1)

            run = {"newton": newton, "split": split, "project": project, "maxima": maxima,
                   "values": values, "residual": residual, "gate": gate}
            for step, l, b in ORDER:
                if step in run:
                    run[step](l, b)
                if (step, l, b) == ("project", 0, 0):
                    prep_layer1()

            for b in range(B):
                read_out(dve, ("logits", 2, b))
            for t in range(TT):
                i = nc.vector.max(m8[:, t, :], lg[:, t, :])
            i.then_inc(gsteps, 1)
            dve.wait_ge(gsteps, 1)
            for t in range(TT):
                i = nc.vector.max_index(i8[:, t, :], m8[:, t, :], lg[:, t, :])
            i.then_inc(gsteps, 1)
            nc.vector.tensor_tensor(df[:, :], m8[:, :, 0], m8[:, :, 1], ALU.subtract).then_inc(gsteps, 1)
            dve.wait_ge(gsteps, 2)
            for s in range(2):
                i = nc.vector.tensor_copy(i2[:, s, :], i8[:, :, s])
            i.then_inc(gsteps, 1)
            dve.wait_ge(tanh, 1)
            nc.vector.tensor_scalar(wt[:, 0, :], th[:, :], 0.5, 0.5, ALU.mult, ALU.add)
            nc.vector.tensor_scalar(wt[:, 1, :], th[:, :], -0.5, 0.5, ALU.mult, ALU.add).then_inc(gsteps, 1)
            dve.wait_ge(gsteps, 5)
            for s in range(2):
                i = nc.vector.tensor_tensor(eq[:, s, :, :], iota[:, :].rearrange("p (o e) -> p o e", o=1).to_broadcast([P, TT, E]),
                                            i2[:, s, :].rearrange("p (t o) -> p t o", o=1).to_broadcast([P, TT, E]), ALU.is_equal)
            i.then_inc(gsteps, 1)
            dve.wait_ge(gsteps, 6)
            for s in range(2):
                i = nc.vector.tensor_tensor(eq[:, s, :, :], eq[:, s, :, :],
                                            wt[:, s, :].rearrange("p (t o) -> p t o", o=1).to_broadcast([P, TT, E]), ALU.mult)
            i.then_inc(gsteps, 1)
            dve.wait_ge(gsteps, 7)
            ev = eq[:, :, :, :].rearrange("p s (a j) e -> p s a j e", a=2)
            for a in range(2):
                i = nc.vector.tensor_tensor(wd[:, :, a, :], ev[:, 0, a, :, :], ev[:, 1, a, :, :], ALU.add)
            i.then_inc(gsteps, 1)
            dve.wait_ge(wt_hi, 1)
            nc.vector.tensor_tensor(wT[:, 1, :], ps("gate_t", p1=2 * E), f32(wT[:, 0, :]), ALU.subtract).then_inc(free_of("gate_t"), 1)

            for e in range(E):
                filled(dve, ("y", e))
                read_out(dve, ("w", e))
                if e >= 2:
                    dve.wait_ge(summed, e)
                nc.vector.scalar_tensor_tensor(yw[:, e % 2, :], ps(("y", e)), b2c[:, e:e + 1], wc[:, e % 2, :],
                                               ALU.add, ALU.mult).then_inc(free_of(("y", e)), 1)
            dve.wait_ge(summed, E)
            read_out(dve, ("y", E - 1))
            nc.vector.tensor_tensor(acc[:, :], acc[:, :], yw[:, (E - 1) % 2, :], ALU.add).then_inc(result, 1)

        @block.tensor
        def _(pe):
            mm = nc.tensor.matmul
            pe.wait_ge(consts, 10)
            pe.wait_ge(stats, 2)
            mm(ps("group", 0, 2 * B), pair[:, :], mv[:, :, :].rearrange("p b s -> p (b s)"), start=True, stop=True).then_inc(full_of("group"), 1)
            pe.wait_ge(prep_v, 1)
            for h in range(H):
                mm(ps(("prep_m", h), 0, P), wg0[D0 * h:D0 * h + D0, 0, :, :].rearrange("p r c -> p (r c)"),
                       wg0[D0 * h:D0 * h + D0, 1, :, :].rearrange("p r c -> p (r c)"), start=True,
                   stop=True).then_inc(full_of(("prep_m", h)), 1)
            pe.wait_ge(ld["g"], 16 * 5)
            nc.tensor.transpose(ps("prep_t", 0, P), wg0[:, 2, :, :].rearrange("p r c -> p (r c)"), ident[:, :])
            nc.tensor.transpose(ps("prep_t", P, 2 * P), wo0[:, :], ident[:, :])
            nc.tensor.transpose(ps("prep_t", 2 * P, 2 * P + NK), b1_raw[:, :], ident[0:NK, 0:NK])
            nc.tensor.transpose(ps("prep_t", 3 * P, 3 * P + E), b2_raw[:, :, :].rearrange("p r c -> p (r c)"),
                                ident[0:E, 0:E]).then_inc(full_of("prep_t"), 1)

            def center(l, b):
                key = ("norm", l, b)
                claim(pe, key)
                if l:
                    pe.wait_ge(cst, 5)
                    read_out(pe, ("o", l - 1, b))
                    mm(ps(key, 0, T), centering[:, :], X[:, b, :], start=True, stop=True).then_inc(S["dev", l], 1)

            def scale(l, b):
                key = ("norm", l, b)
                pe.wait_ge(S["sq", l], b + 1)
                mm(ps(key, T, 2 * T), avg[:, :], sq[:, b, :], start=True, stop=True).then_inc(full_of(key), 1)

            def project(l, b):
                pe.wait_ge(S["X1", l], b + 1)
                pe.wait_ge(S["X2", l], b + 1)
                for u in range(2):
                    key = (f"y{u}", l, b)
                    claim(pe, key)
                    if b == 0 and l == 0:
                        for v in range(2):
                            pe.wait_ge(free_of(("prep_m", 2 * u + v)), 1)
                    elif b == 0:
                        pe.wait_ge(prep_g, 4)
                    for v in range(2):
                        o = ps(key, T * v, T * v + T)
                        if l == 0:
                            w = m_st[:, 2 * u + v, :]
                            mm(o, w, X1[:, b, :], start=True, stop=False)
                            i = mm(o, w, X2[:, b, :], start=False, stop=True)
                        else:
                            heads = slice(H * u + 2 * v, H * u + 2 * v + 2)
                            w, bias = (w_qk[:, s, heads, :, :].rearrange("p h r d -> p (h r d)") for s in range(2))
                            mm(o, w, X1[:, b, :], start=True, stop=False)
                            mm(o, w, X2[:, b, :], start=False, stop=False)
                            i = mm(o, bias, onesr[:, :], start=False, stop=True)
                    i.then_inc(full_of(key), 1)
                key = ("v", l, b)
                claim(pe, key)
                if l == 0 and b == 0:
                    pe.wait_ge(free_of("prep_t"), 1)
                if l:
                    mm(ps(key, 0, KT * C).rearrange("p (t c) -> p t c", t=KT), onesr[:, 0:P],
                       both(w_st[:, 1, 2 * C:3 * C]), start=True, stop=False)
                for t in range(KT):
                    tok = slice(P * t, P * t + P)
                    if l == 0:
                        o = ps(key, P * t, P * t + P)
                        mm(o, X1[:, b, tok], v_st[:, :], start=True, stop=False)
                        i = mm(o, X2[:, b, tok], v_st[:, :], start=False, stop=True)
                    else:
                        o = ps(key, C * t, C * t + C)
                        mm(o, X1[:, b, tok], w_st[:, 0, 2 * C:3 * C], start=False, stop=False)
                        i = mm(o, X2[:, b, tok], w_st[:, 0, 2 * C:3 * C], start=False, stop=(t == KT - 1))
                i.then_inc(full_of(key), 1)

            def q1(b, h, t0, t1):
                p = C * (h % 2)
                return Y[p:p + C, b, 0, T * (h // 2) + t0:T * (h // 2) + t1]

            def k1(b, h, t0, t1):
                p = C * (h % 2)
                return Y[p:p + C, b, 1, T * (h // 2) + t0:T * (h // 2) + t1]

            def both(ap):
                return ap.rearrange("p (o t) -> p o t", o=1).to_broadcast([P, 2, ap.shape[-1]])

            def maxima(l, b):
                if l == 0:
                    for h in range(H):
                        key = (f"s{h}", l, b)
                        claim(pe, key)
                        if h % 2 == 0:
                            read_out(pe, (f"y{h // 2}", l, b))
                        for q in range(KT):
                            c = T * (h % 2) + P * q
                            i = mm(ps(key, T * q, T * q + T), Y[:, b, h // 2, c:c + P], X1[:, b, :], start=True, stop=True)
                        i.then_inc(full_of(key), 1)
                    return
                read_out(pe, ("y0", l, b))
                read_out(pe, ("y1", l, b))
                for u in range(4):
                    key = (f"s{u}", l, b)
                    claim(pe, key)
                    q, n = u // 2, P * (u // 2 + 1)
                    for v in range(2):
                        h = u % 2 + 2 * v
                        mm(ps(key, n * v, n * v + n), q1(b, h, P * q, P * q + P), k1(b, h, 0, n), start=(v == 0), stop=False)
                    o = ps(key, 0, 2 * n).rearrange("p (v t) -> p v t", v=2)[:, :, n - P:n]
                    mm(o, identb[:, :], both(cmask[:, 0, :]), start=False, stop=True).then_inc(full_of(key), 1)

            def probs(l, b):
                if l == 0:
                    for h in range(H):
                        key = (f"t{h}", l, b)
                        claim(pe, key)
                        pe.wait_ge(S["diag", l], 8 * b + 2 * h + 2)
                        y = Y[:, b, h // 2, T * (h % 2):T * (h % 2) + T]
                        mm(ps(key).rearrange("p (t q) -> p t q", t=KT), onesr[:, 0:P],
                           both(diag[:, b, h, :, :].rearrange("p q c -> p (q c)")), start=True, stop=False)
                        for t in range(KT):
                            tok = slice(P * t, P * t + P)
                            o = ps(key, T * t, T * t + T)
                            mm(o, X1[:, b, tok], y, start=False, stop=False)
                            i = mm(o, X2[:, b, tok], y, start=False, stop=(t == KT - 1))
                        i.then_inc(full_of(key), 1)
                    return
                for u in range(4):
                    key = (f"t{u}", l, b)
                    claim(pe, key)
                    pe.wait_ge(S["diag", l], 8 * b + (6, 8, 8, 8)[u])
                    k0 = P * (u // 2)
                    n = T - k0
                    o = ps(key, 0, 2 * n).rearrange("p (v q) -> p v q", v=2)
                    maxes = diag[:, b, :, u // 2:KT, :].rearrange("p (v r) q c -> p r v (q c)", r=2)[:, u % 2, :, :]
                    mm(o, onesr[:, 0:P], maxes, start=True, stop=False)
                    mm(o[:, :, 0:P], identb[:, :], both(cmask[:, 1, :]), start=False, stop=False)
                    for v in range(2):
                        h = u % 2 + 2 * v
                        i = mm(ps(key, n * v, n * v + n), k1(b, h, k0, k0 + P), q1(b, h, k0, T), start=False, stop=(v == 1))
                    i.then_inc(full_of(key), 1)

            def values(l, b):
                for u in range(4):
                    read_out(pe, (f"t{u}", l, b))
                read_out(pe, ("v", l, b))
                key = ("pv", l, b)
                claim(pe, key)
                for den in range(2):
                    for t in range(KT):
                        for h in range(H):
                            if l == 0:
                                w, p, q0 = V0[:, b, t, D0 * h:D0 * h + D0], pr[:, b, 512 * h + T * t:512 * h + T * t + T], 0
                            elif t == 0:
                                c = 512 * (h % 2) + T * (h // 2)
                                w, p, q0 = V1[:, b, t, h, :], pr[:, b, c:c + T], 0
                            else:
                                c = 1024 + T * (h % 2) + P * (h // 2)
                                w, p, q0 = V1[:, b, t, h, :], pr[:, b, c:c + P], P
                            if den:
                                w = onesf[:, :]
                            i = mm(ps(key, T * den + q0, T * den + T, 32 * h, 32 * h + 32), w, p,
                                   start=(t == 0), stop=(t == KT - 1))
                i.then_inc(full_of(key), 1)

            def residual(l, b):
                key = ("o", l, b)
                claim(pe, key)
                if b == 0 and l == 1:
                    pe.wait_ge(ld["b"], 16 * (4 + 2 * H))
                pe.wait_ge(S["att", l], b + 1)
                w = wo0t[:, :] if l == 0 else wo1t[:, :, :].rearrange("p r c -> p (r c)")
                mm(ps(key, 0, T), w, att[:, b, :], start=True, stop=True).then_inc(full_of(key), 1)

            def gate(l, b):
                key = ("logits", l, b)
                claim(pe, key)
                pe.wait_ge(S["X1", l], b + 1)
                for t in range(KT):
                    tok, o = slice(P * t, P * t + P), ps(key, E * t, E * t + E)
                    mm(o, X1[:, b, tok], w_st[:, 0, 3 * C:NW], start=True, stop=False)
                    if t == 0:
                        pe.wait_ge(S["X2", l], b + 1)
                    i = mm(o, X2[:, b, tok], w_st[:, 0, 3 * C:NW], start=False, stop=True)
                i.then_inc(full_of(key), 1)

            run = {"center": center, "scale": scale, "project": project, "maxima": maxima, "probs": probs,
                   "values": values, "residual": residual, "gate": gate}
            def up(k, halves=(0, 1)):
                key = ("h", k)
                if halves[0] == 0:
                    claim(pe, key)
                for s in halves:
                    if k < 2:
                        pe.wait_ge(S["X2", 2], 2 * (s + 1))
                        if s:
                            pe.wait_ge(free[use[key][0] + 1], ring_used[use[key][0] + 1])
                    w = w1_st[:, P * k:P * k + P]
                    o = bank[:, use[key][0] + s, :]
                    x1, x2 = (G[:, 2 * s:2 * s + 2, :].rearrange("p b t -> p (b t)") for G in (X1, X2))
                    mm(o, w, x1, start=True, stop=False)
                    i = mm(o, w, x2, start=False, stop=True)
                if halves[-1] == 1:
                    i.then_inc(full_of(key), 1)

            for step, l, b in ORDER:
                if (step, b) == ("gate", 2):
                    assert all(use["logits", 2, c][0] > 3 for c in (2, 3)) and ORDER[-2:] == [("gate", 2, 2), ("gate", 2, 3)]
                    pe.wait_ge(prep_g, 12)
                    up(0, (0,))
                    up(1, (0,))
                if step in run:
                    run[step](l, b)

            def down(k):
                e, j = divmod(k, FT)
                key = ("y", e)
                if j == 0:
                    claim(pe, key)
                read_out(pe, ("h", k))
                for s in range(2):
                    i = mm(ps(key, p0=C * s, p1=C * s + C), w2_sb[:, k, :], hid[:, k % 3, s, :],
                           start=(j == 0), stop=(j == FT - 1))
                i.then_inc(*((full_of(key), 1) if j == FT - 1 else (hused, 1)))

            def spread(e):
                key = ("w", e)
                claim(pe, key)
                if e == 0:
                    pe.wait_ge(free_of("gate_t"), use["gate_t"][1] + 1)
                w = sel[:, e, :, :].rearrange("p s c -> p (s c)")
                mm(ps(key), w, wT[:, 0, :], start=True, stop=False)
                mm(ps(key), w, wT[:, 1, :], start=False, stop=True).then_inc(full_of(key), 1)

            up(0, (1,))
            up(1, (1,))
            pe.wait_ge(ld["w2"], 16)
            for k in range(NK):
                if 2 <= k + 1 < NK:
                    up(k + 1)
                if k == 1:
                    claim(pe, "gate_t")
                    pe.wait_ge(gsteps, 8)
                    for j in range(TT // 2):
                        i = nc.tensor.transpose(ps("gate_t", P * j, P * j + P, p1=2 * E),
                                                wd[:, j, :, :].rearrange("p s e -> p (s e)"), ident[:, :])
                    i.then_inc(full_of("gate_t"), 1)
                for e in range(E):
                    if SPREAD_AT[e] == k:
                        spread(e)
                down(k)


_INS = ['x', 'L0_conv_g', 'L0_conv_w_qkv', 'L0_conv_w_out', 'L0_conv_b_out', 'L1_attn_W_qkv', 'L1_attn_b_qkv',
        'L1_attn_W_out', 'L1_attn_b_out', 'L1_ffn_Wg', 'L1_ffn_bg', 'L1_ffn_W1', 'L1_ffn_b1', 'L1_ffn_W2', 'L1_ffn_b2']
_OUTS = [((4, 64, 16, 16), 'float32')]


def kernel(**inputs):
    import numpy as _np
    import concourse.bacc as _bacc
    from concourse import mybir as _mybir
    from concourse.bass_utils import run_bass_kernel_spmd as _run

    nc = _bacc.Bacc("TRN2", target_bir_lowering=False, num_devices=1)
    arrays, args = {}, []
    for name in _INS:
        a = _np.ascontiguousarray(inputs[name])
        arrays[f"in_{name}_dram"] = a
        args.append(nc.dram_tensor(f"in_{name}_dram", a.shape, _mybir.dt.from_np(a.dtype), kind="ExternalInput").ap())
    for i, (shape, dtype) in enumerate(_OUTS):
        dt = _mybir.dt.from_np(_np.dtype(dtype))
        args.append(nc.dram_tensor(f"out_{i}_dram", shape, dt, kind="ExternalOutput").ap())
    hybrid_block(nc, *args)
    r = _run(nc, [arrays], core_ids=[0])
    return r.results[0]["out_0_dram"]
```
